# Optimizing a Trainium2 kernel written in Bass

```python
import numpy as np
import jax
import jax.numpy as jnp

def _softmax(x, axis=-1):
    return jax.nn.softmax(x, axis=axis)

def _gelu(x):
    return jax.nn.gelu(x, approximate=True)

def _silu(x):
    return jax.nn.silu(x)

def _sigmoid(x):
    return jax.nn.sigmoid(x)

def _layernorm(x, axis=-1, eps=1e-05):
    m = jnp.mean(x, axis=axis, keepdims=True)
    v = jnp.var(x, axis=axis, keepdims=True)
    return (x - m) / jnp.sqrt(v + eps)

def _scatter_add(tgt, idx, src, axis=0):
    return tgt.at[idx].add(src)

def _segment_sum(src, seg, n):
    return jax.ops.segment_sum(src, seg, n)
kernel_name = 'mk_adaln_attn_ffn_d1_seqx_r8_e46ab3'

def setup_inputs(seed: int=0):
    np.random.seed(seed)
    _w = jnp.asarray

    def _rec_inputs():
        import jax
        import jax.numpy as jnp
        _rk = jax.random.key(seed)
        x = -7.109e-05 + 0.9999 * jax.random.normal(jax.random.fold_in(_rk, 1), (32, 32, 512), jnp.float32)
        _lenS = 32 - jax.random.randint(jax.random.fold_in(_rk, 7), (32,), 0, max(1, 32 // 4) + 1, jnp.int32)
        _lenS2 = 32 - jax.random.randint(jax.random.fold_in(_rk, 8), (32,), 0, max(1, 32 // 4) + 1, jnp.int32)
        itok_B_0_15 = jax.random.randint(jax.random.fold_in(_rk, 11), (32,), 0, 16, jnp.int32)
        return (x, itok_B_0_15)
    x, itok_B_0_15 = _rec_inputs()

    def _L0_cond_setup():
        import jax, jax.numpy as jnp
        import numpy as np
        NUM_CONDITIONS = 16
        IN_CH = 32
        OUT_CH = 32
        B = 64
        T = 512
        key = jax.random.key(seed)
        k_x, k_w, k_c = jax.random.split(key, 3)
        x = jax.random.normal(k_x, (B, IN_CH, T), dtype=jnp.float32)
        bound = float(np.sqrt(6.0 / IN_CH))
        weights = jax.random.uniform(k_w, (NUM_CONDITIONS, IN_CH, OUT_CH), dtype=jnp.float32, minval=-bound, maxval=bound)
        condition = jax.random.randint(k_c, (B,), 0, NUM_CONDITIONS, dtype=jnp.int64)
        return {'x': x, 'weights': weights, 'condition': condition}
    _L0_cond_all = _L0_cond_setup()
    _L0_cond_in = {k: v for k, v in _L0_cond_all.items() if k in ('weights',)}
    del _L0_cond_all

    def _L0_attn_setup():
        import jax, jax.numpy as jnp
        import numpy as np
        H, KV, HD, HID = (32, 8, 128, 512)
        THETA, FACTOR, HI_FF, LO_FF, ORIG_MAX = (500000.0, 8.0, 4.0, 1.0, 1024)

        def _llama3_inv_freq():
            inv = 1.0 / THETA ** (np.arange(0, HD, 2, dtype=np.float64) / HD)
            wavelen = 2.0 * np.pi / inv
            low_wl = ORIG_MAX / LO_FF
            high_wl = ORIG_MAX / HI_FF
            smooth = (ORIG_MAX / wavelen - LO_FF) / (HI_FF - LO_FF)
            scaled = np.where(wavelen > low_wl, inv / FACTOR, inv)
            mid = (wavelen <= low_wl) & (wavelen >= high_wl)
            scaled = np.where(mid, (1 - smooth) * inv / FACTOR + smooth * inv, scaled)
            return scaled.astype(np.float32)

        def _rope_cos_sin(T):
            inv = _llama3_inv_freq()
            pos = np.arange(T, dtype=np.float32)
            freqs = pos[:, None] * inv[None, :]
            emb = np.concatenate([freqs, freqs], axis=-1)
            return (jnp.asarray(np.cos(emb)), jnp.asarray(np.sin(emb)))

        def _rotate_half(x):
            x1, x2 = jnp.split(x, 2, axis=-1)
            return jnp.concatenate([-x2, x1], axis=-1)
        key = jax.random.key(seed)
        ks = jax.random.split(key, 5)
        s = 1.0 / np.sqrt(HID)
        return {'x': jax.random.normal(ks[0], (1, 256, HID), jnp.float32), 'wq': jax.random.normal(ks[1], (HID, H * HD), jnp.float32) * s, 'wk': jax.random.normal(ks[2], (HID, KV * HD), jnp.float32) * s, 'wv': jax.random.normal(ks[3], (HID, KV * HD), jnp.float32) * s, 'wo': jax.random.normal(ks[4], (H * HD, HID), jnp.float32) * s}
    _L0_attn_all = _L0_attn_setup()
    _L0_attn_in = {k: v for k, v in _L0_attn_all.items() if k in ('wq', 'wk', 'wv', 'wo')}
    del _L0_attn_all

    def _L0_cond2_setup():
        import jax, jax.numpy as jnp
        import numpy as np
        B, C, T = (64, 32, 512)
        S, D = (16, 32)
        key = jax.random.key(seed)
        k1, k2, k3 = jax.random.split(key, 3)
        x = jax.random.normal(k1, (B, C, T), dtype=jnp.float32)
        condition = jax.random.randint(k2, (B,), 0, S, dtype=jnp.int64)
        bound = float(np.sqrt(6.0 / C))
        weights = jax.random.uniform(k3, (S, C, D), dtype=jnp.float32, minval=-bound, maxval=bound)
        return {'x': x, 'condition': condition, 'weights': weights}
    _L0_cond2_all = _L0_cond2_setup()
    _L0_cond2_in = {k: v for k, v in _L0_cond2_all.items() if k in ('weights',)}
    del _L0_cond2_all

    def _L0_ffn_setup():
        import jax, jax.numpy as jnp
        import numpy as np
        FP8_MAX = 448.0

        def per_tensor_quantize(t):
            amax = jnp.max(jnp.abs(t))
            scale = jnp.maximum(amax, 1e-12) / FP8_MAX
            q = jnp.clip(t / scale, -FP8_MAX, FP8_MAX)
            return (q, scale.astype(jnp.float32))

        def fp8_cast(t):
            rounded = t.astype(jnp.float8_e4m3fn).astype(t.dtype)
            return t + jax.lax.stop_gradient(rounded - t)
        key = jax.random.key(seed)
        k1, k2, k3 = jax.random.split(key, 3)
        B, S, D_IN, D_OUT = (4, 256, 512, 512)
        x = jax.random.normal(k1, (B, S, D_IN), dtype=jnp.float32)
        w = jax.random.normal(k2, (D_OUT, D_IN), dtype=jnp.float32) * 0.02
        qweight, weight_scale = per_tensor_quantize(w)
        bias = jax.random.normal(k3, (D_OUT,), dtype=jnp.float32) * 0.01
        return {'x': x, 'qweight': qweight, 'weight_scale': weight_scale, 'bias': bias}
    _L0_ffn_all = _L0_ffn_setup()
    _L0_ffn_in = {k: v for k, v in _L0_ffn_all.items() if k in ('qweight', 'weight_scale', 'bias')}
    del _L0_ffn_all
    return {'x': x, 'itok_B_0_15': itok_B_0_15, 'L0_cond_weights': _L0_cond_in['weights'], 'L0_attn_wq': _L0_attn_in['wq'], 'L0_attn_wk': _L0_attn_in['wk'], 'L0_attn_wv': _L0_attn_in['wv'], 'L0_attn_wo': _L0_attn_in['wo'], 'L0_cond2_weights': _L0_cond2_in['weights'], 'L0_ffn_qweight': _L0_ffn_in['qweight'], 'L0_ffn_weight_scale': _L0_ffn_in['weight_scale'], 'L0_ffn_bias': _L0_ffn_in['bias']}

def reference(x, itok_B_0_15, L0_cond_weights, L0_attn_wq, L0_attn_wk, L0_attn_wv, L0_attn_wo, L0_cond2_weights, L0_ffn_qweight, L0_ffn_weight_scale, L0_ffn_bias):
    import jax
    import jax.numpy as jnp

    def _L0_cond_ref(x, weights, condition):
        import jax, jax.numpy as jnp
        import numpy as np
        NUM_CONDITIONS = 16
        IN_CH = 32
        OUT_CH = 32
        B = 64
        T = 512
        W = weights[condition]
        return jnp.einsum('bct,bcd->bdt', x, W)

    def _L0_attn_ref(x, wq, wk, wv, wo):
        import jax, jax.numpy as jnp
        import numpy as np
        H, KV, HD, HID = (32, 8, 128, 512)
        THETA, FACTOR, HI_FF, LO_FF, ORIG_MAX = (500000.0, 8.0, 4.0, 1.0, 1024)

        def _llama3_inv_freq():
            inv = 1.0 / THETA ** (np.arange(0, HD, 2, dtype=np.float64) / HD)
            wavelen = 2.0 * np.pi / inv
            low_wl = ORIG_MAX / LO_FF
            high_wl = ORIG_MAX / HI_FF
            smooth = (ORIG_MAX / wavelen - LO_FF) / (HI_FF - LO_FF)
            scaled = np.where(wavelen > low_wl, inv / FACTOR, inv)
            mid = (wavelen <= low_wl) & (wavelen >= high_wl)
            scaled = np.where(mid, (1 - smooth) * inv / FACTOR + smooth * inv, scaled)
            return scaled.astype(np.float32)

        def _rope_cos_sin(T):
            inv = _llama3_inv_freq()
            pos = np.arange(T, dtype=np.float32)
            freqs = pos[:, None] * inv[None, :]
            emb = np.concatenate([freqs, freqs], axis=-1)
            return (jnp.asarray(np.cos(emb)), jnp.asarray(np.sin(emb)))

        def _rotate_half(x):
            x1, x2 = jnp.split(x, 2, axis=-1)
            return jnp.concatenate([-x2, x1], axis=-1)
        B, T, _ = x.shape
        q = (x @ wq).reshape(B, T, H, HD).transpose(0, 2, 1, 3)
        k = (x @ wk).reshape(B, T, KV, HD).transpose(0, 2, 1, 3)
        v = (x @ wv).reshape(B, T, KV, HD).transpose(0, 2, 1, 3)
        cos, sin = _rope_cos_sin(T)
        q = q * cos + _rotate_half(q) * sin
        k = k * cos + _rotate_half(k) * sin
        rep = H // KV
        k = jnp.repeat(k, rep, axis=1)
        v = jnp.repeat(v, rep, axis=1)
        scores = jnp.einsum('bhtd,bhsd->bhts', q, k) * (1.0 / np.sqrt(HD))
        mask = jnp.tril(jnp.ones((T, T), dtype=bool))
        scores = jnp.where(mask, scores, -jnp.inf)
        att = jax.nn.softmax(scores, axis=-1)
        out = jnp.einsum('bhts,bhsd->bhtd', att, v)
        out = out.transpose(0, 2, 1, 3).reshape(B, T, H * HD)
        return out @ wo

    def _L0_cond2_ref(x, condition, weights):
        import jax, jax.numpy as jnp
        import numpy as np
        B, C, T = (64, 32, 512)
        S, D = (16, 32)
        W = weights[condition]
        return jnp.einsum('bct,bcd->bdt', x, W)

    def _L0_ffn_ref(x, qweight, weight_scale, bias):
        import jax, jax.numpy as jnp
        import numpy as np
        FP8_MAX = 448.0

        def per_tensor_quantize(t):
            amax = jnp.max(jnp.abs(t))
            scale = jnp.maximum(amax, 1e-12) / FP8_MAX
            q = jnp.clip(t / scale, -FP8_MAX, FP8_MAX)
            return (q, scale.astype(jnp.float32))

        def fp8_cast(t):
            rounded = t.astype(jnp.float8_e4m3fn).astype(t.dtype)
            return t + jax.lax.stop_gradient(rounded - t)
        quantize_output = True
        qinput, input_scale = per_tensor_quantize(x)
        qinput = fp8_cast(qinput)
        qw = fp8_cast(qweight)
        a = qinput * input_scale.astype(x.dtype)
        b = qw * weight_scale.astype(x.dtype)
        out = jnp.einsum('bsd,od->bso', a, b) + bias
        if quantize_output:
            qout, out_scale = per_tensor_quantize(out)
            out = qout * out_scale
        return out
    x = x + _L0_attn_ref(_L0_cond_ref(x, L0_cond_weights, itok_B_0_15), L0_attn_wq, L0_attn_wk, L0_attn_wv, L0_attn_wo)
    x = x + _L0_ffn_ref(_L0_cond2_ref(x, itok_B_0_15, L0_cond2_weights), L0_ffn_qweight, L0_ffn_weight_scale, L0_ffn_bias)
    return x

_drawn_inputs = setup_inputs


def setup_inputs(seed=0):
    import zlib

    import numpy as np

    out = dict(_drawn_inputs(seed))
    spreads = {}
    factors = {'L0_ffn_bias': 8.0}
    for name, (base, spread) in spreads.items():
        noise = np.random.default_rng([zlib.crc32(name.encode()), seed]).standard_normal(out[name].shape)
        drawn = base * np.exp(spread * noise) if base else spread * noise
        out[name] = jnp.asarray(drawn.astype(out[name].dtype))
    for name, factor in factors.items():
        out[name] = (out[name] * factor).astype(out[name].dtype)
    return out
```

```python
from contextlib import ExitStack

import numpy as np

import concourse.bass as bass
from concourse import mybir

F32 = mybir.dt.float32
F32R = mybir.dt.float32r
BF16 = mybir.dt.bfloat16
I32 = mybir.dt.int32
ALU = mybir.AluOpType
ACT = mybir.ActivationFunctionType
AX_X = mybir.AxisListType.X

P = 128
BATCH, T, HID = 32, 32, 512
HEADS, KV, HD = 32, 8, 128
CONDS = 16
REP = HEADS // KV
ROWS = BATCH * T
TILES = ROWS // P
BPT = P // T
KC = HID // P
HALF = ROWS // 2
TPU = TILES // 2
BPU = HALF // T
ITEMS = 1 + REP
SCALE = 1.0 / float(np.sqrt(HD))
MASKED = -1.0e30
FP8_MAX = 448.0
EXP_BITS = 0x7F800000
HALF_BIT = 0x00400000
SHIFT = float(2 ** 20)
LEAST = 1.5 * 2.0 ** 14

C_COS, C_SIN, C_SVAL, C_CSEL, C_BLOCK, C_IDENT, C_TRI, C_ONE = 0, 32, 64, 68, 100, 104, 232, 360
C_WIDTH = C_ONE + P
ITEM_BANK = [0, 1, 2, 0, 1]


def constant_table():
    theta, factor, hi_ff, lo_ff, orig_max = 500000.0, 8.0, 4.0, 1.0, 1024
    inv = 1.0 / theta ** (np.arange(0, HD, 2, dtype=np.float64) / HD)
    wavelen = 2.0 * np.pi / inv
    low_wl, high_wl = orig_max / lo_ff, orig_max / hi_ff
    smooth = (orig_max / wavelen - lo_ff) / (hi_ff - lo_ff)
    scaled = np.where(wavelen > low_wl, inv / factor, inv)
    mid = (wavelen <= low_wl) & (wavelen >= high_wl)
    scaled = np.where(mid, (1 - smooth) * inv / factor + smooth * inv, scaled).astype(np.float32)
    freqs = np.arange(T, dtype=np.float32)[:, None] * scaled[None, :]
    emb = np.concatenate([freqs, freqs], axis=-1)
    sign = np.where(np.arange(HD) < HD // 2, -1.0, 1.0).astype(np.float32)
    part = np.arange(P)
    table = np.zeros((P, C_WIDTH), np.float32)
    table[:, C_COS:C_COS + T] = np.cos(emb).T
    table[:, C_SIN:C_SIN + T] = np.sin(emb).T * sign[:, None]
    table[:, C_SVAL:C_SVAL + 4] = (P // T) * np.arange(4)[None, :] + part[:, None] // T
    table[:, C_CSEL:C_CSEL + T] = part[:, None] % T == np.arange(T)[None, :]
    table[:, C_BLOCK:C_BLOCK + 4] = part[:, None] // T == np.arange(4)[None, :]
    table[:, C_IDENT:C_IDENT + P] = np.eye(P)
    table[:T, C_TRI:C_TRI + P] = np.where(part[None, :] % T > np.arange(T)[:, None], MASKED, 0.0)
    table[0, C_ONE:C_ONE + P] = 1.0
    return table


def build(nc, x, itok, cond_w, wq, wk, wv, wo, cond2_w, qweight, w_scale, bias, consts, out):
    with ExitStack() as ctx:
        def sb(name, shape, dt=F32):
            return ctx.enter_context(nc.sbuf_tensor(name, shape, dt))

        def sem(name):
            return ctx.enter_context(nc.semaphore(name))

        cst = sb("cst", [P, C_WIDTH])
        ident_bf = sb("ident_bf", [P, P], BF16)
        tri_bf = sb("tri_bf", [P, P], BF16)
        pos_bf = sb("pos_bf", [P, TPU * REP, T], BF16)
        xacc = sb("xacc", [P, TILES, HID])
        hT_hi = sb("hT_hi", [P, KC, ROWS], F32R)
        hT_lo = sb("hT_lo", [P, KC, ROWS], F32R)
        v_all = sb("v_all", [P, TILES, KV * HD])
        wq_hi = sb("wq_hi", [P, KC, REP * HD], F32R)
        wq_lo = sb("wq_lo", [P, KC, REP * HD], F32R)
        wk_hi = sb("wk_hi", [P, KC, HD], F32R)
        wk_lo = sb("wk_lo", [P, KC, HD], F32R)
        wo_hi = sb("wo_hi", [P, REP, HID], F32R)
        wo_lo = sb("wo_lo", [P, REP, HID], F32R)
        raw_q = sb("raw_q", [P, KC, REP * HD])
        raw_k = sb("raw_k", [P, KC, HD])
        raw_o = sb("raw_o", [P, REP, HID])
        o_hi = sb("o_hi", [P, TPU, REP * P], F32R)
        o_lo = sb("o_lo", [P, TPU, REP * P], F32R)
        q_rot = sb("q_rot", [P, REP, HALF])
        k_rot = sb("k_rot", [P, HALF])
        q_cos = [sb(f"q_cos{i}", [P, HALF]) for i in range(2)]
        q_swap = [sb(f"q_swap{i}", [P, HALF]) for i in range(2)]
        s_nat = sb("s_nat", [P, TPU * REP, T])
        s_exp = sb("s_exp", [P, TPU * REP, T])
        p_tr = sb("p_tr", [P, TPU * REP, T])
        s_max = sb("s_max", [P, TPU * REP])
        s_sum = sb("s_sum", [P, TPU * REP])
        s_rec = sb("s_rec", [P, TPU * REP])
        pb_hi = sb("pb_hi", [P, TPU * REP, BPT, T], F32R)
        pb_lo = sb("pb_lo", [P, TPU * REP, BPT, T], F32R)
        v_hi = sb("v_hi", [P, TPU, HD], F32R)
        v_lo = sb("v_lo", [P, TPU, HD], F32R)
        wbd2 = sb("wbd2", [P, TILES, BPT, T])
        tok_i = sb("tok_i", [P, BATCH], I32)
        tok_f = sb("tok_f", [P, BATCH])
        tok_eq = sb("tok_eq", [P, 4, BATCH])
        wT = sb("wT", [P, KC, HID], BF16)
        wsc = sb("wsc", [P, 1])
        y_max = sb("y_max", [P, TILES])
        f_max = sb("f_max", [P, TILES])
        col = sb("col", [P, 12])
        row = sb("row", [1, 4])

        bank = [ctx.enter_context(nc.psum_tensor(f"bank{i}", [P, 512], F32)) for i in range(8)]
        q_ps = bank[0:3]
        s_ps = bank[3]
        o_ps = bank[4:6]
        w_ps = bank[6:8]

        dma_const, dma_x, dma_cond, dma_wv, dma_ffn = (sem(n) for n in ("dma_const", "dma_x", "dma_cond", "dma_wv", "dma_ffn"))
        dma_qk, dma_o, dma_out = sem("dma_qk"), sem("dma_o"), sem("dma_out")
        const_done = sem("const_done")
        tok_step, sel_lhs, sel_mm, wbd_done = sem("tok_step"), sem("sel_lhs"), sem("sel_mm"), sem("wbd_done")
        h_mm, h_hi_done, h_lo_done = sem("h_mm"), sem("h_hi_done"), sem("h_lo_done")
        wv_hi_done, wv_lo_done, v_mm, v_copied = sem("wv_hi_done"), sem("wv_lo_done"), sem("v_mm"), sem("v_copied")
        w8_scaled, w8_step, wT_mm, wT_done = sem("w8_scaled"), sem("w8_step"), sem("wT_mm"), sem("wT_done")
        qk_hi_done, qk_lo_done, wo_hi_done, wo_lo_done = (sem(n) for n in ("qk_hi_done", "qk_lo_done", "wo_hi_done", "wo_lo_done"))
        proj_mm, swap_done, rope_mul, rope_done = sem("proj_mm"), sem("swap_done"), sem("rope_mul"), sem("rope_done")
        scores_mm, soft_step, exp_done = sem("scores_mm"), sem("soft_step"), sem("exp_done")
        p_hi_done, p_lo_done, v_hi_done, v_lo_done = (sem(n) for n in ("p_hi_done", "p_lo_done", "v_hi_done", "v_lo_done"))
        pv_mm, o_hi_done, o_lo_done, wo_mm, acc_done = (sem(n) for n in ("pv_mm", "o_hi_done", "o_lo_done", "wo_mm", "acc_done"))
        y_mm, y_copied, y_amax, tail_mm, tail_vec = (sem(n) for n in ("y_mm", "y_copied", "y_amax", "tail_mm", "tail_vec"))
        y_scaled, y8_step, f_mm, f_done, f_div, f_clip, result = (sem(n) for n in ("y_scaled", "y8_step", "f_mm", "f_done", "f_div", "f_clip", "result"))

        x_rows = x.rearrange("(j b) c h -> j (b c) h", b=BPT)
        out_rows = out.rearrange("(j b) c h -> j (b c) h", b=BPT)
        wq_v = wq.rearrange("(c p) n -> p c n", p=P)
        wk_v = wk.rearrange("(c p) n -> p c n", p=P)
        wv_v = wv.rearrange("(c p) n -> p c n", p=P)
        wo_v = wo.rearrange("(h p) n -> p h n", p=P)
        qw_v = qweight.rearrange("(c p) n -> p c n", p=P)
        cond_v = cond_w.rearrange("(k s) c d -> (s c) k d", k=4)
        cond2_v = cond2_w.rearrange("(k s) c d -> (s c) k d", k=4)
        cos_b = cst[:, C_COS:C_COS + T].unsqueeze(1).broadcast_to([P, BPU, T])
        sin_b = cst[:, C_SIN:C_SIN + T].unsqueeze(1).broadcast_to([P, BPU, T])
        ident = cst[:, C_IDENT:C_IDENT + P]
        csel_b = cst[:, C_CSEL:C_CSEL + T].unsqueeze(1).unsqueeze(1).broadcast_to([P, 4, BPT, T])
        block_b = cst[:, C_BLOCK:C_BLOCK + BPT].unsqueeze(1).unsqueeze(3).broadcast_to([P, TPU, BPT, T])
        sel_buf = [q_cos[0], q_cos[1]]
        wbd1 = [a[:].rearrange("p (t b d) -> p t b d", t=TPU, b=BPT) for a in q_swap]
        wcond = k_rot[:, 0:4 * 2 * T].rearrange("p (k n) -> p k n", k=4)
        w8 = lambda c: q_cos[c // 2][:].bitcast(BF16)[:, (c % 2) * HID:(c % 2 + 1) * HID]
        y8 = q_rot[:].bitcast(BF16).rearrange("p h (a n) -> p (h a) n", a=2)
        bias_b = raw_k[:].rearrange("p c n -> p (c n)")
        by_t = lambda a: a.rearrange("p (b t) -> p b t", t=T)
        y_t = lambda t: (raw_q if t < TPU else raw_o)[:, t % TPU, :]
        tmp_scaled = [s_nat[:].rearrange("p a t -> p (a t)"), s_exp[:].rearrange("p a t -> p (a t)")]
        tmp_sum = p_tr[:].rearrange("p a t -> p (a t)")

        block = ctx.enter_context(nc.Block())

        @block.sync
        def _(sp):
            sp.dma_start(cst[:], consts).then_inc(dma_const, 16)
            sp.dma_start(xacc[:, 0, :], x_rows[0]).then_inc(dma_x, 16)
            for t in range(1, TILES):
                sp.wait_ge(dma_x, 16 * t)
                sp.dma_start(xacc[:, t, :], x_rows[t]).then_inc(dma_x, 16)
                if t == 2:
                    sp.dma_start(raw_o[:], wv_v[:, :, 0:512]).then_inc(dma_wv, 16)
            sp.wait_ge(dma_wv, 16)
            sp.dma_start(raw_q[:], wv_v[:, :, 512:1024]).then_inc(dma_wv, 16)
            sp.dma_start(raw_k[:], wk_v[:, :, 0:HD]).then_inc(dma_qk, 16)
            sp.dma_start(q_rot[:], qw_v).then_inc(dma_ffn, 16)

            def load_weights(g):
                if isinstance(g, int) and g == 0:
                    sp.wait_ge(wv_lo_done, 2 * KC)
                else:
                    sp.wait_ge(qk_lo_done, g * ITEMS)
                    sp.dma_start(raw_k[:], wk_v[:, :, bass.ds(g * HD, HD)]).then_inc(dma_qk, 16)
                sp.dma_start(raw_q[:], wq_v[:, :, bass.ds(g * REP * HD, REP * HD)]).then_inc(dma_qk, 16)
                if not (isinstance(g, int) and g == 0):
                    sp.wait_ge(wo_lo_done, g * REP)
                sp.dma_start(raw_o[:], wo_v[:, bass.ds(g * REP, REP), :]).then_inc(dma_o, 16)

            load_weights(0)
            with sp.Fori(1, KV) as g:
                load_weights(g)
            sp.wait_ge(qk_lo_done, KV * ITEMS)
            sp.dma_start(bias_b, bias.unsqueeze(0).broadcast_to([P, HID])).then_inc(dma_ffn, 16)
            for t in range(TILES):
                sp.wait_ge(result, t + 1)
                sp.dma_start(out_rows[t], xacc[:, t, :]).then_inc(dma_out, 16)
            sp.wait_ge(dma_out, 16 * TILES)

        @block.gpsimd
        def _(pool):
            pool.memset(pb_hi[:].bitcast(F32), 0.0)
            pool.memset(pb_lo[:].bitcast(F32), 0.0).then_inc(const_done, 1)

            def qk_lo(g):
                for k in range(ITEMS):
                    pool.wait_ge(qk_hi_done, g * ITEMS + k + 1)
                    raw, hi, lo = ((raw_k[:], wk_hi[:], wk_lo[:]) if k == 0 else
                                   (w[:, :, (k - 1) * HD:k * HD] for w in (raw_q, wq_hi, wq_lo)))
                    pool.tensor_tensor(lo, raw, hi.bitcast(F32), ALU.subtract).then_inc(qk_lo_done, 1)

            def wo_lo_split(g):
                for h in range(REP):
                    pool.wait_ge(wo_hi_done, g * REP + h + 1)
                    pool.tensor_tensor(wo_lo[:, h, :], raw_o[:, h, :], wo_hi[:, h, :].bitcast(F32),
                                       ALU.subtract).then_inc(wo_lo_done, 1)

            def v_low(g, r):
                u = 2 * g + r
                pool.wait_ge(v_hi_done, u + 1)
                pool.tensor_tensor(v_lo[:], v_all[:, r * TPU:(r + 1) * TPU, bass.ds(g * HD, HD)],
                                   v_hi[:].bitcast(F32), ALU.subtract).then_inc(v_lo_done, 1)

            def rope_add(g, r, k):
                n = 2 * ITEMS * g + ITEMS * r + k
                b = (ITEMS * r + k) % 2
                pool.wait_ge(rope_mul, n + 1)
                if not (isinstance(g, int) and 2 * g + r == 0):
                    pool.wait_ge(scores_mm, 2 * g + r)
                else:
                    pool.wait_ge(wT_done, 1)
                dst = k_rot[:] if k == 0 else q_rot[:, k - 1, :]
                pool.tensor_tensor(dst, q_cos[b][:], q_swap[b][:], ALU.add).then_inc(rope_done, 1)

            for c in range(2 * KC):
                raw, hi, lo = ((raw_o, wo_hi, wo_lo) if c < KC else (raw_q, o_hi, o_lo))
                pool.wait_ge(wv_hi_done, c + 1)
                pool.tensor_tensor(lo[:, c % KC, :], raw[:, c % KC, :], hi[:, c % KC, :].bitcast(F32),
                                   ALU.subtract).then_inc(wv_lo_done, 1)
            qk_lo(0)
            wo_lo_split(0)

            def group(g, first=False, last=False):
                if not first:
                    v_low(g - 1, 1)
                for k in range(ITEMS):
                    rope_add(g, 0, k)
                v_low(g, 0)
                for k in range(ITEMS):
                    rope_add(g, 1, k)
                if not first:
                    wo_lo_split(g)
                if not last:
                    qk_lo(g + 1)

            group(0, first=True)
            with pool.Fori(1, KV - 1) as g:
                group(g)
            group(KV - 1, last=True)
            v_low(KV - 1, 1)

        @block.scalar
        def _(act):
            act.dma_start(tok_i[:], itok.unsqueeze(0).broadcast_to([P, BATCH])).then_inc(dma_cond, 16)
            act.dma_start(wcond[:, :, 0:T], cond_v).then_inc(dma_cond, 16)
            act.dma_start(wcond[:, :, T:2 * T], cond2_v).then_inc(dma_cond, 16)
            act.dma_start(wsc[:], w_scale.broadcast_to([P, 1])).then_inc(dma_cond, 16)
            act.wait_ge(dma_const, 16)
            act.activation(ident_bf[:], ident, ACT.Copy).then_inc(const_done, 1)
            act.activation(tri_bf[:], cst[:, C_TRI:C_TRI + P], ACT.Copy).then_inc(const_done, 1)
            act.activation(pos_bf[:], cst[:, C_IDENT:C_IDENT + T].unsqueeze(1).broadcast_to([P, TPU * REP, T]),
                           ACT.Copy).then_inc(const_done, 1)

            def h_high(t):
                act.wait_ge(h_mm, t + 1)
                act.activation(hT_hi[:, :, t * P:(t + 1) * P], q_ps[t % 2][:].rearrange("p (c r) -> p c r", c=KC),
                               ACT.Copy).then_inc(h_hi_done, 1)

            def wv_high(c):
                raw, hi = (raw_o, wo_hi) if c < KC else (raw_q, o_hi)
                act.wait_ge(dma_wv, 16 if c < KC else 32)
                act.activation(hi[:, c % KC, :], raw[:, c % KC, :], ACT.Copy).then_inc(wv_hi_done, 1)

            for c in range(KC):
                wv_high(c)
            for t in range(TILES):
                h_high(t)
            for c in range(KC, 2 * KC):
                wv_high(c)
            for c in range(KC):
                act.wait_ge(dma_ffn, 16)
                if c >= 2:
                    act.wait_ge(w8_step, 3 * (c - 1))
                act.activation(tmp_scaled[c % 2], q_rot[:, c, :], ACT.Copy, scale=SHIFT).then_inc(w8_scaled, 1)

            def qk_high(g):
                act.wait_ge(dma_qk, 32 * (g + 1))
                for k in range(ITEMS):
                    if not (isinstance(g, int) and g == 0):
                        act.wait_ge(proj_mm, 2 * ITEMS * g - ITEMS + k + 1)
                    raw, hi = ((raw_k[:], wk_hi[:]) if k == 0 else
                               (w[:, :, (k - 1) * HD:k * HD] for w in (raw_q, wq_hi)))
                    act.activation(hi, raw, ACT.Copy).then_inc(qk_hi_done, 1)

            def wo_high(g):
                act.wait_ge(dma_o, 16 * (g + 1))
                if isinstance(g, int) and g == 0:
                    act.wait_ge(v_mm, TILES)
                else:
                    act.wait_ge(wo_mm, 2 * TPU * g)
                for h in range(REP):
                    act.activation(wo_hi[:, h, :], raw_o[:, h, :], ACT.Copy).then_inc(wo_hi_done, 1)

            def swap(g, r, k):
                n = 2 * ITEMS * g + ITEMS * r + k
                b = (ITEMS * r + k) % 2
                act.wait_ge(proj_mm, n + 1)
                if not (isinstance(g, int) and 2 * g + r == 0 and k < 2):
                    act.wait_ge(rope_done, n - 1)
                ps = q_ps[ITEM_BANK[k]]
                act.activation(q_swap[b][0:P // 2, :], ps[P // 2:P, :], ACT.Copy)
                act.activation(q_swap[b][P // 2:P, :], ps[0:P // 2, :], ACT.Copy).then_inc(swap_done, 1)

            def v_high(g, r):
                u = 2 * g + r
                if not (isinstance(g, int) and u == 0):
                    act.wait_ge(pv_mm, TPU * u)
                else:
                    act.wait_ge(v_copied, 2 * TILES)
                act.activation(v_hi[:], v_all[:, r * TPU:(r + 1) * TPU, bass.ds(g * HD, HD)],
                               ACT.Copy).then_inc(v_hi_done, 1)

            def exponent(g, r):
                u = 2 * g + r
                act.wait_ge(soft_step, 7 * u + 3)
                act.activation(s_exp[:], s_nat[:], ACT.Exp, scale=SCALE).then_inc(exp_done, 1)

            def p_high(g, r):
                u = 2 * g + r
                act.wait_ge(soft_step, 7 * u + 7)
                if isinstance(g, int) and u == 0:
                    act.wait_ge(const_done, 4)
                else:
                    act.wait_ge(pv_mm, TPU * u)
                for b in range(BPT):
                    s = slice(T * b, T * b + T)
                    act.activation(pb_hi[s, :, b, :], p_tr[s, :, :], ACT.Copy).then_inc(p_hi_done, 1)

            def o_high(g, r, j):
                u = 2 * g + r
                act.wait_ge(pv_mm, TPU * u + j + 1)
                if not (isinstance(g, int) and u == 0):
                    act.wait_ge(wo_mm, TPU * u - TPU + j + 1)
                elif j == 0:
                    act.wait_ge(v_mm, 2 * TILES)
                act.activation(o_hi[:, j, :], o_ps[j % 2][:], ACT.Copy).then_inc(o_hi_done, 1)

            def softmax_and_swaps(last, cur):
                if last is not None:
                    v_high(*last)
                if cur is not None:
                    swap(*cur, 0)
                if last is not None:
                    exponent(*last)
                if cur is not None:
                    swap(*cur, 1)
                    swap(*cur, 2)
                if last is not None:
                    p_high(*last)
                if cur is not None:
                    swap(*cur, 3)
                    swap(*cur, 4)

            def outputs(last):
                for j in range(TPU):
                    o_high(*last, j)

            qk_high(0)
            wo_high(0)

            def group(g, first=False, last=False):
                softmax_and_swaps(None if first else (g - 1, 1), (g, 0))
                if not first:
                    outputs((g - 1, 1))
                softmax_and_swaps((g, 0), (g, 1))
                if not first:
                    wo_high(g)
                if not last:
                    qk_high(g + 1)
                outputs((g, 0))

            group(0, first=True)
            with act.Fori(1, KV - 1) as g:
                group(g)
            group(KV - 1, last=True)
            softmax_and_swaps((KV - 1, 1), None)
            outputs((KV - 1, 1))

            def y_copy(t):
                act.wait_ge(y_mm, t + 1)
                if t == 0:
                    act.wait_ge(qk_lo_done, KV * ITEMS)
                    act.wait_ge(wo_lo_done, KV * REP)
                act.activation(y_t(t), q_ps[t % 3][:], ACT.Copy).then_inc(y_copied, 1)

            for t in range(TILES):
                y_copy(t)
            for t in range(TILES):
                if t == 0:
                    act.wait_ge(tail_vec, 5)
                else:
                    act.wait_ge(y8_step, 3 * (t - 1) + 1 if t < 2 else 3 * (t - 1))
                act.activation(tmp_scaled[t % 2], y_t(t), ACT.Copy, scale=col[:, 2:3]).then_inc(y_scaled, 1)
                if t >= 2:
                    act.wait_ge(y8_step, 3 * (t - 1))
                act.activation(q_swap[t % 2][:], y_t(t), ACT.Copy, scale=col[:, 1:2]).then_inc(y_scaled, 1)
            for t in range(TILES):
                act.wait_ge(tail_vec, 10)
                act.activation(v_all[:, t, 0:HID], v_all[:, t, HID:2 * HID], ACT.Copy,
                               scale=col[:, 6:7]).then_inc(f_div, 1)

        @block.tensor
        def _(pe):
            pe.wait_ge(dma_cond, 64)
            for t in range(TILES):
                pe.wait_ge(sel_lhs, t + 1)
                lhs = sel_buf[t % 2][:].rearrange("p (k m) -> p k m", k=4)
                for k in range(4):
                    mm = pe.matmul(s_ps[:, t * 64:(t + 1) * 64], lhs[:, k, :], wcond[:, k, :],
                                   start=(k == 0), stop=(k == 3))
                mm.then_inc(sel_mm, 1)
            pe.wait_ge(wbd_done, 2)
            for t in range(TILES):
                pe.wait_ge(dma_x, 16 * (t + 1))
                if t >= 2:
                    pe.wait_ge(h_lo_done, t - 1)
                for c in range(KC):
                    mm = pe.matmul(q_ps[t % 2][:, c * P:(c + 1) * P], xacc[:, t, c * P:(c + 1) * P],
                                   wbd1[t // TPU][:, t % TPU, :, :], start=True, stop=True)
                mm.then_inc(h_mm, 1)

            def three_pass(dst, pairs, first_wait=None):
                n = len(pairs)
                for i, ((l_hi, l_lo), (r_hi, r_lo)) in enumerate(pairs):
                    pe.matmul(dst, l_hi, r_hi, start=(i == 0), stop=False)
                    pe.matmul(dst, l_hi, r_lo, start=False, stop=False)
                    mm = pe.matmul(dst, l_lo, r_hi, start=False, stop=(i == n - 1))
                return mm

            for n in range(2):
                hi, lo = (wo_hi, wo_lo) if n == 0 else (o_hi, o_lo)
                for t in range(TILES):
                    if t == 0:
                        pe.wait_ge(wv_lo_done, KC * (n + 1))
                    pe.wait_ge(h_lo_done, t + 1)
                    i = n * TILES + t
                    if i >= 2:
                        pe.wait_ge(v_copied, i - 1)
                    rows = slice(t * P, (t + 1) * P)
                    three_pass(w_ps[i % 2][:], [((hT_hi[:, c, rows], hT_lo[:, c, rows]), (hi[:, c, :], lo[:, c, :]))
                                                for c in range(KC)]).then_inc(v_mm, 1)
            for c in range(KC):
                pe.wait_ge(w8_step, 3 * (c + 1))
                pe.wait_ge(const_done, 4)
                dst = o_ps[c // 2][:].bitcast(BF16)
                for d in range(KC):
                    mm = pe.transpose(dst[:, (c % 2) * 512 + d * P:(c % 2) * 512 + (d + 1) * P],
                                      w8(c)[:, d * P:(d + 1) * P], ident_bf[:])
                if c % 2:
                    mm.then_inc(wT_mm, 1)

            def project(g, r):
                u = 2 * g + r
                zero = isinstance(g, int) and u == 0
                rows = slice(r * HALF, (r + 1) * HALF)
                for k in range(ITEMS):
                    n = 2 * ITEMS * g + ITEMS * r + k
                    if r == 0:
                        pe.wait_ge(qk_lo_done, g * ITEMS + k + 1)
                    if not zero:
                        pe.wait_ge(rope_mul, n - 2 if k in (0, 1) else (n - 4 if k == 2 else n - 2))
                    elif k >= 3:
                        pe.wait_ge(rope_mul, n - 2)
                    w = (wk_hi, wk_lo) if k == 0 else (wq_hi, wq_lo)
                    cols = slice(0, HD) if k == 0 else slice((k - 1) * HD, k * HD)
                    three_pass(q_ps[ITEM_BANK[k]][:],
                               [((w[0][:, c, cols], w[1][:, c, cols]), (hT_hi[:, c, rows], hT_lo[:, c, rows]))
                                for c in range(KC)]).then_inc(proj_mm, 1)

            def scores(g, r):
                u = 2 * g + r
                if not (isinstance(g, int) and u == 0):
                    pe.wait_ge(soft_step, 7 * u - 6)
                else:
                    pe.wait_ge(const_done, 4)
                pe.matmul(s_ps[:], tri_bf[:], pos_bf[:], start=True, stop=False, skip_group_check=True)
                pe.wait_ge(rope_done, ITEMS * (u + 1))
                for j in range(TPU):
                    for b in range(BPT):
                        cols = slice((j * BPT + b) * T, (j * BPT + b + 1) * T)
                        mm = pe.matmul(s_ps[T * b:T * (b + 1), j * P:(j + 1) * P], k_rot[:, cols], q_rot[:, :, cols],
                                       start=False, stop=True, skip_group_check=True)
                mm.then_inc(scores_mm, 1)

            def attend(g, r, j):
                u = 2 * g + r
                if j == 0:
                    pe.wait_ge(p_lo_done, BPT * (u + 1))
                    pe.wait_ge(v_lo_done, u + 1)
                if not (isinstance(g, int) and u == 0 and j < 2):
                    pe.wait_ge(o_lo_done, TPU * u + j - 1)
                elif j == 0:
                    pe.wait_ge(wT_done, 1)
                heads = slice(j * REP, (j + 1) * REP)
                three_pass(o_ps[j % 2][:], [((v_hi[:, j, :], v_lo[:, j, :]),
                                             (pb_hi[:, heads, :, :], pb_lo[:, heads, :, :]))]).then_inc(pv_mm, 1)

            def project_out(g, r, j):
                u = 2 * g + r
                if j == 0:
                    pe.wait_ge(wo_lo_done, REP * (g + 1))
                pe.wait_ge(o_lo_done, TPU * u + j + 1)
                if not (isinstance(g, int) and u == 0 and j < 2):
                    pe.wait_ge(acc_done, TPU * u + j - 1)
                elif j == 0:
                    pe.wait_ge(v_copied, 2 * TILES)
                three_pass(w_ps[j % 2][:],
                           [((o_hi[:, j, h * P:(h + 1) * P], o_lo[:, j, h * P:(h + 1) * P]),
                             (wo_hi[:, h, :], wo_lo[:, h, :])) for h in range(REP)]).then_inc(wo_mm, 1)

            def attend_and_out(g, r):
                attend(g, r, 0)
                attend(g, r, 1)
                for j in range(TPU):
                    project_out(g, r, j)
                    if j + 2 < TPU:
                        attend(g, r, j + 2)

            def group(g, first=False):
                project(g, 0)
                if not first:
                    attend_and_out(g - 1, 1)
                scores(g, 0)
                project(g, 1)
                attend_and_out(g, 0)
                scores(g, 1)

            group(0, first=True)
            with pe.Fori(1, KV) as g:
                group(g)

            def mix2(t):
                pe.wait_ge(acc_done, TPU * 2 * (KV - 1) + t + 1)
                pe.wait_ge(rope_mul, 2 * ITEMS * KV)
                if t >= 3:
                    pe.wait_ge(y_copied, t - 2)
                for c in range(KC):
                    mm = pe.matmul(q_ps[t % 3][:, c * P:(c + 1) * P], xacc[:, t, c * P:(c + 1) * P],
                                   wbd2[:, t, :, :], start=True, stop=True)
                mm.then_inc(y_mm, 1)

            for t in range(TPU - 1):
                mix2(t)
            attend_and_out(KV - 1, 1)
            for t in range(TPU - 1, TILES):
                mix2(t)

            def spread_max(n):
                pe.wait_ge(tail_vec, 5 * n + 1)
                pe.transpose(s_ps[0:1, 0:P], col[:, 4 * n:4 * n + 1], ident).then_inc(tail_mm, 1)
                pe.wait_ge(tail_vec, 5 * n + 2)
                pe.matmul(s_ps[:, P:P + 1], cst[0:1, C_ONE:C_ONE + P], row[0:1, n:n + 1],
                          start=True, stop=True).then_inc(tail_mm, 1)

            spread_max(0)
            for t in range(TILES):
                pe.wait_ge(y8_step, 3 * (t + 1))
                if t >= 2:
                    pe.wait_ge(f_done, 2 * (t - 1) - 1)
                for c in range(KC):
                    mm = pe.matmul(w_ps[t % 2][:], y8[:, t, c * P:(c + 1) * P], wT[:, c, :],
                                   start=(c == 0), stop=(c == KC - 1))
                mm.then_inc(f_mm, 1)
            spread_max(1)

        @block.vector
        def _(dve):
            dve.wait_ge(dma_cond, 64)
            dve.wait_ge(dma_const, 16)
            dve.tensor_copy(tok_f[:], tok_i[:]).then_inc(tok_step, 1)
            dve.wait_ge(tok_step, 1)
            for k in range(4):
                dve.tensor_scalar(tok_eq[:, k, :], tok_f[:], cst[:, C_SVAL + k:C_SVAL + k + 1], None,
                                  ALU.is_equal).then_inc(tok_step, 1)
            dve.wait_ge(tok_step, 5)
            for t in range(TILES):
                if t >= 2:
                    dve.wait_ge(sel_mm, t - 1)
                eq_b = tok_eq[:, :, t * BPT:(t + 1) * BPT].unsqueeze(3).broadcast_to([P, 4, BPT, T])
                dve.tensor_tensor(sel_buf[t % 2][:].rearrange("p (k b c) -> p k b c", k=4, b=BPT), eq_b, csel_b,
                                  ALU.mult).then_inc(sel_lhs, 1)
            dve.wait_ge(sel_mm, TILES)
            picked = s_ps[:].rearrange("p (t w d) -> p t w d", w=2, d=T)
            for w, half, dst in ((0, 0, wbd1[0]), (0, 1, wbd1[1]), (1, 0, wbd2[:, 0:TPU]), (1, 1, wbd2[:, TPU:TILES])):
                src = picked[:, half * TPU:(half + 1) * TPU, w, :]
                dve.tensor_tensor(dst, src.unsqueeze(2).broadcast_to([P, TPU, BPT, T]), block_b,
                                  ALU.mult).then_inc(wbd_done, 1)

            def h_low(t):
                dve.wait_ge(h_hi_done, t + 1)
                cols = slice(t * P, (t + 1) * P)
                dve.tensor_tensor(hT_lo[:, :, cols], q_ps[t % 2][:].rearrange("p (c r) -> p c r", c=KC),
                                  hT_hi[:, :, cols].bitcast(F32), ALU.subtract).then_inc(h_lo_done, 1)

            for t in range(TILES):
                h_low(t)

            def round_e4m3(dst, scaled, plain, total, done, n):
                dve.tensor_scalar(scaled.bitcast(I32), scaled.bitcast(I32), EXP_BITS, HALF_BIT,
                                  ALU.bitwise_and, ALU.bitwise_or).then_inc(done, 1)
                dve.wait_ge(done, 3 * n + 1)
                dve.scalar_tensor_tensor(out=total, in0=scaled, scalar=LEAST, in1=plain, op0=ALU.max,
                                         op1=ALU.add).then_inc(done, 1)
                dve.wait_ge(done, 3 * n + 2)
                dve.scalar_tensor_tensor(out=dst, in0=scaled, scalar=LEAST, in1=total, op0=ALU.max,
                                         op1=ALU.subtract).then_inc(done, 1)

            def v_copy(i):
                n, t = divmod(i, TILES)
                dve.wait_ge(v_mm, i + 1)
                dve.tensor_copy(v_all[:, t, n * 512:(n + 1) * 512], w_ps[i % 2][:]).then_inc(v_copied, 1)

            for i in range(TILES):
                v_copy(i)
            for c in range(KC):
                dve.wait_ge(w8_scaled, c + 1)
                round_e4m3(w8(c), tmp_scaled[c % 2], q_rot[:, c, :], tmp_sum, w8_step, c)
                v_copy(TILES + 2 * c)
                v_copy(TILES + 2 * c + 1)
            for h in range(2):
                dve.wait_ge(wT_mm, h + 1)
                src = o_ps[h][:].bitcast(BF16).rearrange("p (a c o) -> p a c o", a=2, c=KC)
                mm = dve.tensor_copy(wT[:, :, h * 256:(h + 1) * 256].rearrange("p c (a o) -> p a c o", a=2), src)
            mm.then_inc(wT_done, 1)

            def rope(g, r, k):
                n = 2 * ITEMS * g + ITEMS * r + k
                b = (ITEMS * r + k) % 2
                dve.wait_ge(swap_done, n + 1)
                if not (isinstance(g, int) and 2 * g + r == 0 and k < 2):
                    dve.wait_ge(rope_done, n - 1)
                dve.tensor_tensor(by_t(q_swap[b][:]), by_t(q_swap[b][:]), sin_b, ALU.mult)
                dve.tensor_tensor(by_t(q_cos[b][:]), by_t(q_ps[ITEM_BANK[k]][:]), cos_b,
                                  ALU.mult).then_inc(rope_mul, 1)

            def soft(g, r, step):
                u = 2 * g + r
                if step == 0:
                    dve.wait_ge(scores_mm, u + 1)
                elif step != 3:
                    dve.wait_ge(soft_step, 7 * u + step)
                if step == 0:
                    op = dve.transpose(s_nat[:].rearrange("p a t -> p (a t)"), s_ps[:])
                elif step == 1:
                    op = dve.tensor_reduce(s_max[:], s_nat[:], AX_X, ALU.max)
                elif step == 2:
                    op = dve.tensor_tensor(s_nat[:], s_nat[:], s_max[:].unsqueeze(2).broadcast_to([P, TPU * REP, T]),
                                           ALU.subtract)
                elif step == 3:
                    dve.wait_ge(exp_done, u + 1)
                    op = dve.tensor_reduce(s_sum[:], s_exp[:], AX_X, ALU.add)
                elif step == 4:
                    op = dve.reciprocal(s_rec[:], s_sum[:])
                elif step == 5:
                    op = dve.tensor_tensor(s_nat[:], s_exp[:], s_rec[:].unsqueeze(2).broadcast_to([P, TPU * REP, T]),
                                           ALU.mult)
                elif step == 6:
                    if not (isinstance(g, int) and u == 0):
                        dve.wait_ge(p_hi_done, BPT * u)
                    op = dve.transpose(p_tr[:].rearrange("p a t -> p (a t)"), s_nat[:].rearrange("p a t -> p (a t)"))
                op.then_inc(soft_step, 1)

            def p_low(g, r):
                u = 2 * g + r
                for b in range(BPT):
                    s = slice(T * b, T * b + T)
                    dve.wait_ge(p_hi_done, BPT * u + b + 1)
                    if b == 0 and not (isinstance(g, int) and u == 0):
                        dve.wait_ge(pv_mm, TPU * u)
                    dve.tensor_tensor(pb_lo[s, :, b, :], p_tr[s, :, :], pb_hi[s, :, b, :].bitcast(F32),
                                      ALU.subtract).then_inc(p_lo_done, 1)

            def o_low(g, r, j):
                u = 2 * g + r
                dve.wait_ge(o_hi_done, TPU * u + j + 1)
                dve.tensor_tensor(o_lo[:, j, :], o_ps[j % 2][:], o_hi[:, j, :].bitcast(F32),
                                  ALU.subtract).then_inc(o_lo_done, 1)

            def accumulate(g, r, j):
                u = 2 * g + r
                tile = r * TPU + j
                dve.wait_ge(wo_mm, TPU * u + j + 1)
                if not (isinstance(g, int) and g == 0):
                    dve.wait_ge(acc_done, TPU * u - TPU)
                dve.tensor_tensor(xacc[:, tile, :], xacc[:, tile, :], w_ps[j % 2][:], ALU.add).then_inc(acc_done, 1)

            def softmax_and_ropes(last, cur):
                if last is not None:
                    soft(*last, 0)
                    soft(*last, 1)
                    soft(*last, 2)
                if cur is not None:
                    rope(*cur, 0)
                if last is not None:
                    for step in range(3, 7):
                        soft(*last, step)
                if cur is not None:
                    rope(*cur, 1)
                    rope(*cur, 2)
                if last is not None:
                    p_low(*last)
                if cur is not None:
                    rope(*cur, 3)
                    rope(*cur, 4)

            def outputs(last):
                o_low(*last, 0)
                o_low(*last, 1)
                for j in range(TPU):
                    accumulate(*last, j)
                    if j + 2 < TPU:
                        o_low(*last, j + 2)

            def group(g, first=False):
                softmax_and_ropes(None if first else (g - 1, 1), (g, 0))
                if not first:
                    outputs((g - 1, 1))
                softmax_and_ropes((g, 0), (g, 1))
                outputs((g, 0))

            group(0, first=True)
            with dve.Fori(1, KV) as g:
                group(g)
            softmax_and_ropes((KV - 1, 1), None)
            outputs((KV - 1, 1))

            for t in range(TILES):
                dve.wait_ge(y_copied, t + 1)
                dve.tensor_reduce(y_max[:, t:t + 1], y_t(t), AX_X, ALU.max,
                                  apply_absolute_value=True).then_inc(y_amax, 1)

            def amax_steps(n, per_tile, ready, count):
                dve.wait_ge(ready, count)
                dve.tensor_reduce(col[:, 4 * n:4 * n + 1], per_tile[:], AX_X, ALU.max).then_inc(tail_vec, 1)
                dve.wait_ge(tail_mm, 2 * n + 1)
                dve.tensor_reduce(row[0:1, n:n + 1], s_ps[0:1, 0:P], AX_X, ALU.max).then_inc(tail_vec, 1)
                dve.wait_ge(tail_mm, 2 * n + 2)
                dve.tensor_scalar(col[:, 4 * n + 3:4 * n + 4], s_ps[:, P:P + 1], 1e-12, 1.0 / FP8_MAX, ALU.max,
                                  ALU.mult).then_inc(tail_vec, 1)

            amax_steps(0, y_max, y_amax, TILES)
            dve.wait_ge(tail_vec, 3)
            dve.reciprocal(col[:, 1:2], col[:, 3:4]).then_inc(tail_vec, 1)
            dve.tensor_scalar(col[:, 8:9], col[:, 3:4], wsc[:, 0:1], None, ALU.mult)
            dve.wait_ge(tail_vec, 4)
            dve.tensor_scalar(col[:, 2:3], col[:, 1:2], SHIFT, None, ALU.mult).then_inc(tail_vec, 1)

            dve.wait_ge(dma_ffn, 32)

            def f_take(t):
                dve.wait_ge(f_mm, t + 1)
                f = v_all[:, t, HID:2 * HID]
                dve.scalar_tensor_tensor(out=f, in0=w_ps[t % 2][:], scalar=col[:, 8:9], in1=bias_b,
                                         op0=ALU.mult, op1=ALU.add).then_inc(f_done, 1)
                dve.wait_ge(f_done, 2 * t + 1)
                dve.tensor_reduce(f_max[:, t:t + 1], f, AX_X, ALU.max,
                                  apply_absolute_value=True).then_inc(f_done, 1)

            for t in range(TILES):
                dve.wait_ge(y_scaled, 2 * (t + 1))
                round_e4m3(y8[:, t, :], tmp_scaled[t % 2], q_swap[t % 2][:], tmp_sum, y8_step, t)
                if t >= 1:
                    f_take(t - 1)
            f_take(TILES - 1)
            amax_steps(1, f_max, f_done, 2 * TILES)
            dve.wait_ge(tail_vec, 8)
            dve.reciprocal(col[:, 6:7], col[:, 7:8]).then_inc(tail_vec, 1)
            dve.wait_ge(tail_vec, 9)
            dve.tensor_copy(col[:, 9:10], col[:, 7:8]).then_inc(tail_vec, 1)
            dve.wait_ge(tail_vec, 10)
            for t in range(TILES):
                f = v_all[:, t, 0:HID]
                dve.wait_ge(f_div, t + 1)
                dve.tensor_scalar(f, f, FP8_MAX, -FP8_MAX, ALU.min, ALU.max).then_inc(f_clip, 1)
                dve.wait_ge(f_clip, t + 1)
                dve.scalar_tensor_tensor(out=xacc[:, t, :], in0=f, scalar=col[:, 9:10], in1=xacc[:, t, :],
                                         op0=ALU.mult, op1=ALU.add).then_inc(result, 1)


_INS = ["x", "itok_B_0_15", "L0_cond_weights", "L0_attn_wq", "L0_attn_wk", "L0_attn_wv", "L0_attn_wo",
        "L0_cond2_weights", "L0_ffn_qweight", "L0_ffn_weight_scale", "L0_ffn_bias"]


def kernel(**inputs):
    import concourse.bacc as bacc
    from concourse.bass_utils import run_bass_kernel_spmd

    nc = bacc.Bacc("TRN2", target_bir_lowering=False, num_devices=1)
    arrays, args = {}, []
    for name in _INS:
        a = np.ascontiguousarray(inputs[name])
        if a.ndim == 0:
            a = a.reshape(1)
        arrays[f"in_{name}"] = a
    arrays["in_constants"] = constant_table()
    for name, a in arrays.items():
        args.append(nc.dram_tensor(name, a.shape, mybir.dt.from_np(a.dtype), kind="ExternalInput").ap())
    out = nc.dram_tensor("out_0", (BATCH, T, HID), F32, kind="ExternalOutput").ap()
    build(nc, *args, out)
    r = run_bass_kernel_spmd(nc, [arrays], core_ids=[0])
    return r.results[0]["out_0"]
```

```python
from contextlib import ExitStack

import numpy as np

import concourse.bass as bass
from concourse import mybir

F32 = mybir.dt.float32
F32R = mybir.dt.float32r
BF16 = mybir.dt.bfloat16
I32 = mybir.dt.int32
ALU = mybir.AluOpType
ACT = mybir.ActivationFunctionType
AX_X = mybir.AxisListType.X

P = 128
BATCH, T, HID = 32, 32, 512
HEADS, KV, HD = 32, 8, 128
CONDS = 16
REP = HEADS // KV
ROWS = BATCH * T
TILES = ROWS // P
BPT = P // T
KC = HID // P
HALF = ROWS // 2
TPU = TILES // 2
BPU = HALF // T
ITEMS = 1 + REP
SCALE = 1.0 / float(np.sqrt(HD))
MASKED = -1.0e30
FP8_MAX = 448.0
EXP_BITS = 0x7F800000
HALF_BIT = 0x00400000
SHIFT = float(2 ** 20)
LEAST = 1.5 * 2.0 ** 14

C_COS, C_SIN, C_SVAL, C_CSEL, C_BLOCK, C_IDENT, C_TRI, C_ONE = 0, 32, 64, 68, 100, 104, 232, 360
C_WIDTH = C_ONE + P
V_LATE = 2
ITEM_BANK = [0, 1, 2, 0, 1]


def constant_table():
    theta, factor, hi_ff, lo_ff, orig_max = 500000.0, 8.0, 4.0, 1.0, 1024
    inv = 1.0 / theta ** (np.arange(0, HD, 2, dtype=np.float64) / HD)
    wavelen = 2.0 * np.pi / inv
    low_wl, high_wl = orig_max / lo_ff, orig_max / hi_ff
    smooth = (orig_max / wavelen - lo_ff) / (hi_ff - lo_ff)
    scaled = np.where(wavelen > low_wl, inv / factor, inv)
    mid = (wavelen <= low_wl) & (wavelen >= high_wl)
    scaled = np.where(mid, (1 - smooth) * inv / factor + smooth * inv, scaled).astype(np.float32)
    freqs = np.arange(T, dtype=np.float32)[:, None] * scaled[None, :]
    emb = np.concatenate([freqs, freqs], axis=-1)
    sign = np.where(np.arange(HD) < HD // 2, -1.0, 1.0).astype(np.float32)
    part = np.arange(P)
    table = np.zeros((P, C_WIDTH), np.float32)
    table[:, C_COS:C_COS + T] = np.cos(emb).T
    table[:, C_SIN:C_SIN + T] = np.sin(emb).T * sign[:, None]
    table[:, C_SVAL:C_SVAL + 4] = (P // T) * np.arange(4)[None, :] + part[:, None] // T
    table[:, C_CSEL:C_CSEL + T] = part[:, None] % T == np.arange(T)[None, :]
    table[:, C_BLOCK:C_BLOCK + 4] = part[:, None] // T == np.arange(4)[None, :]
    table[:, C_IDENT:C_IDENT + P] = np.eye(P)
    table[:T, C_TRI:C_TRI + P] = np.where(part[None, :] % T > np.arange(T)[:, None], MASKED, 0.0)
    table[0, C_ONE:C_ONE + P] = 1.0
    return table


def build(nc, x, itok, cond_w, wq, wk, wv, wo, cond2_w, qweight, w_scale, bias, consts, out):
    with ExitStack() as ctx:
        def sb(name, shape, dt=F32):
            return ctx.enter_context(nc.sbuf_tensor(name, shape, dt))

        def sem(name):
            return ctx.enter_context(nc.semaphore(name))

        cst = sb("cst", [P, C_WIDTH])
        ident_bf = sb("ident_bf", [P, P], BF16)
        tri_bf = sb("tri_bf", [P, P], BF16)
        pos_bf = sb("pos_bf", [P, TPU * REP, T], BF16)
        xacc = sb("xacc", [P, TILES, HID])
        hT_hi = sb("hT_hi", [P, KC, ROWS], F32R)
        hT_lo = sb("hT_lo", [P, KC, ROWS], F32R)
        v_all = sb("v_all", [P, TILES, KV * HD])
        wq_hi = sb("wq_hi", [P, KC, REP * HD], F32R)
        wq_lo = sb("wq_lo", [P, KC, REP * HD], F32R)
        wk_hi = sb("wk_hi", [P, KC, HD], F32R)
        wk_lo = sb("wk_lo", [P, KC, HD], F32R)
        wo_hi = sb("wo_hi", [P, REP, HID], F32R)
        wo_lo = sb("wo_lo", [P, REP, HID], F32R)
        raw_q = sb("raw_q", [P, KC, REP * HD])
        raw_k = sb("raw_k", [P, KC, HD])
        raw_o = sb("raw_o", [P, REP, HID])
        o_hi = sb("o_hi", [P, TPU, REP * P], F32R)
        o_lo = sb("o_lo", [P, TPU, REP * P], F32R)
        q_rot = sb("q_rot", [P, REP, HALF])
        k_rot = sb("k_rot", [P, HALF])
        q_cos = [sb(f"q_cos{i}", [P, HALF]) for i in range(2)]
        q_swap = [sb(f"q_swap{i}", [P, HALF]) for i in range(2)]
        s_nat = sb("s_nat", [P, TPU * REP, T])
        s_exp = sb("s_exp", [P, TPU * REP, T])
        p_tr = sb("p_tr", [P, TPU * REP, T])
        s_max = sb("s_max", [P, TPU * REP])
        s_sum = sb("s_sum", [P, TPU * REP])
        s_rec = sb("s_rec", [P, TPU * REP])
        pb_hi = sb("pb_hi", [P, TPU * REP, BPT, T], F32R)
        pb_lo = sb("pb_lo", [P, TPU * REP, BPT, T], F32R)
        v_hi = sb("v_hi", [P, TPU, HD], F32R)
        v_lo = sb("v_lo", [P, TPU, HD], F32R)
        wbd2 = sb("wbd2", [P, TILES, BPT, T])
        tok_i = sb("tok_i", [P, BATCH], I32)
        tok_f = sb("tok_f", [P, BATCH])
        tok_eq = sb("tok_eq", [P, 4, BATCH])
        wT = sb("wT", [P, KC, HID], BF16)
        wsc = sb("wsc", [P, 1])
        y_max = sb("y_max", [P, TILES])
        f_max = sb("f_max", [P, TILES])
        col = sb("col", [P, 12])
        row = sb("row", [1, 4])

        bank = [ctx.enter_context(nc.psum_tensor(f"bank{i}", [P, 512], F32)) for i in range(8)]
        q_ps = bank[0:3]
        s_ps = bank[3]
        o_ps = bank[4:6]
        w_ps = bank[6:8]

        dma_const, dma_x, dma_cond, dma_wv, dma_ffn = (sem(n) for n in ("dma_const", "dma_x0", "dma_cond", "dma_wv", "dma_ffn"))
        dma_x = [dma_x] + [sem(f"dma_x{i}") for i in range(1, TILES // 2)]
        dma_qk, dma_o, dma_out = sem("dma_qk"), sem("dma_o"), sem("dma_out")
        const_done = sem("const_done")
        tok_step, wc_step, sel_lhs, sel_lhs_pool = sem("tok_step"), sem("wc_step"), sem("sel_lhs"), sem("sel_lhs_pool")
        sel_mm, wbd_done = sem("sel_mm"), sem("wbd_done")
        h_mm, h_hi_done, h_lo_done = sem("h_mm"), sem("h_hi_done"), sem("h_lo_done")
        wv_hi_done, wv_lo_done, v_mm, v_copied = sem("wv_hi_done"), sem("wv_lo_done"), sem("v_mm"), sem("v_copied")
        w8_scaled, w8_step, wT_mm, wT_done = sem("w8_scaled"), sem("w8_step"), sem("wT_mm"), sem("wT_done")
        qk_hi_done, qk_lo_done, wo_hi_done, wo_lo_done = (sem(n) for n in ("qk_hi_done", "qk_lo_done", "wo_hi_done", "wo_lo_done"))
        proj_mm, swap_done, rope_mul, rope_done = sem("proj_mm"), sem("swap_done"), sem("rope_mul"), sem("rope_done")
        scores_mm, soft_step, exp_done = sem("scores_mm"), sem("soft_step"), sem("exp_done")
        p_hi_done, p_lo_done, v_hi_done, v_lo_done = (sem(n) for n in ("p_hi_done", "p_lo_done", "v_hi_done", "v_lo_done"))
        pv_mm, o_hi_done, o_lo_done, wo_mm, acc_done = (sem(n) for n in ("pv_mm", "o_hi_done", "o_lo_done", "wo_mm", "acc_done"))
        y_mm, y_copied, y_amax, tail_mm, tail_vec = (sem(n) for n in ("y_mm", "y_copied", "y_amax", "tail_mm", "tail_vec"))
        y_scaled, y8_step, f_mm, f_done, f_div, f_clip, result = (sem(n) for n in ("y_scaled", "y8_step", "f_mm", "f_done", "f_div", "f_clip", "result"))

        x_rows = x.rearrange("(j b) c h -> j (b c) h", b=BPT)
        out_rows = out.rearrange("(j b) c h -> j (b c) h", b=BPT)
        wq_v = wq.rearrange("(c p) n -> p c n", p=P)
        wk_v = wk.rearrange("(c p) n -> p c n", p=P)
        wv_v = wv.rearrange("(c p) n -> p c n", p=P)
        wo_v = wo.rearrange("(h p) n -> p h n", p=P)
        qw_v = qweight.rearrange("(c p) n -> p c n", p=P)
        cond_v = cond_w.rearrange("(k s) c d -> (s c) k d", k=4)
        cond2_v = cond2_w.rearrange("(k s) c d -> (s c) k d", k=4)
        cos_b = cst[:, C_COS:C_COS + T].unsqueeze(1).broadcast_to([P, BPU, T])
        sin_b = cst[:, C_SIN:C_SIN + T].unsqueeze(1).broadcast_to([P, BPU, T])
        ident = cst[:, C_IDENT:C_IDENT + P]
        csel_b = cst[:, C_CSEL:C_CSEL + T].unsqueeze(1).unsqueeze(1).broadcast_to([P, 4, 2 * BPT, T])
        block_b = cst[:, C_BLOCK:C_BLOCK + BPT].unsqueeze(1).unsqueeze(3).broadcast_to([P, TPU, BPT, T])
        flat = lambda a: a[:].rearrange("p a t -> p (a t)")
        selector = [a.bitcast(BF16).rearrange("p (k b c) -> p k b c", k=4, c=T)
                    for a in (q_cos[0][:], q_cos[1][:], flat(s_nat), flat(s_exp))]
        wc_rest = k_rot[:, 256:512].rearrange("p (k n) -> p k n", k=4)
        wc_part = [flat(p_tr).bitcast(BF16)[:, i * 256:(i + 1) * 256].rearrange("p (k n) -> p k n", k=4)
                   for i in range(3)]
        wbd1 = [a[:].rearrange("p (t b d) -> p t b d", t=TPU, b=BPT) for a in q_swap]
        wcond = k_rot[:, 0:4 * 2 * T].rearrange("p (k n) -> p k n", k=4)
        w8 = lambda c: q_cos[c // 2][:].bitcast(BF16)[:, (c % 2) * HID:(c % 2 + 1) * HID]
        y8 = q_rot[:].bitcast(BF16).rearrange("p h (a n) -> p (h a) n", a=2)
        bias_b = raw_k[:].rearrange("p c n -> p (c n)")
        by_t = lambda a: a.rearrange("p (b t) -> p b t", t=T)
        y_t = lambda t: (raw_q if t < TPU else raw_o)[:, t % TPU, :]
        tmp_scaled = [s_nat[:].rearrange("p a t -> p (a t)"), s_exp[:].rearrange("p a t -> p (a t)")]
        tmp_sum = p_tr[:].rearrange("p a t -> p (a t)")

        def select_pair(eng, i):
            eq_b = tok_eq[:, :, 2 * i * BPT:2 * (i + 1) * BPT].unsqueeze(3).broadcast_to([P, 4, 2 * BPT, T])
            return eng.tensor_tensor(selector[i], eq_b, csel_b, ALU.mult)

        block = ctx.enter_context(nc.Block())

        @block.sync
        def _(sp):
            sp.dma_start(cst[:], consts).then_inc(dma_const, 16)
            for t in range(0, TILES, 2):
                sp.dma_start(xacc[:, t:t + 2, :], x_rows[t:t + 2].rearrange("t p h -> p t h")).then_inc(dma_x[t // 2], 16)
                if t == 2:
                    sp.dma_start(raw_o[:], wv_v[:, :, 0:512]).then_inc(dma_wv, 16)
            sp.wait_ge(dma_wv, 16)
            sp.dma_start(raw_q[:], wv_v[:, :, 512:1024]).then_inc(dma_wv, 16)
            sp.dma_start(raw_k[:], wk_v[:, :, 0:HD]).then_inc(dma_qk, 16)
            sp.dma_start(q_rot[:], qw_v).then_inc(dma_ffn, 16)

            def load_weights(g):
                if isinstance(g, int) and g == 0:
                    sp.wait_ge(wv_lo_done, 2 * KC)
                else:
                    sp.wait_ge(qk_lo_done, g * ITEMS)
                    sp.dma_start(raw_k[:], wk_v[:, :, bass.ds(g * HD, HD)]).then_inc(dma_qk, 16)
                sp.dma_start(raw_q[:], wq_v[:, :, bass.ds(g * REP * HD, REP * HD)]).then_inc(dma_qk, 16)
                if not (isinstance(g, int) and g == 0):
                    sp.wait_ge(wo_lo_done, g * REP)
                sp.dma_start(raw_o[:], wo_v[:, bass.ds(g * REP, REP), :]).then_inc(dma_o, 16)

            load_weights(0)
            with sp.Fori(1, KV) as g:
                load_weights(g)
            sp.wait_ge(qk_lo_done, KV * ITEMS)
            sp.dma_start(bias_b, bias.unsqueeze(0).broadcast_to([P, HID])).then_inc(dma_ffn, 16)
            for t in range(TILES):
                sp.wait_ge(result, t + 1)
                sp.dma_start(out_rows[t], xacc[:, t, :]).then_inc(dma_out, 16)
            sp.wait_ge(dma_out, 16 * TILES)

        @block.gpsimd
        def _(pool):
            pool.memset(pb_hi[:].bitcast(F32), 0.0)
            pool.memset(pb_lo[:].bitcast(F32), 0.0).then_inc(const_done, 1)

            def qk_lo(g):
                for k in range(ITEMS):
                    pool.wait_ge(qk_hi_done, g * ITEMS + k + 1)
                    raw, hi, lo = ((raw_k[:], wk_hi[:], wk_lo[:]) if k == 0 else
                                   (w[:, :, (k - 1) * HD:k * HD] for w in (raw_q, wq_hi, wq_lo)))
                    pool.tensor_tensor(lo, raw, hi.bitcast(F32), ALU.subtract).then_inc(qk_lo_done, 1)

            def wo_lo_split(g, heads):
                for h in heads:
                    pool.wait_ge(wo_hi_done, g * REP + h + 1)
                    pool.tensor_tensor(wo_lo[:, h, :], raw_o[:, h, :], wo_hi[:, h, :].bitcast(F32),
                                       ALU.subtract).then_inc(wo_lo_done, 1)

            def v_low(g, r):
                u = 2 * g + r
                pool.wait_ge(v_hi_done, u + 1)
                pool.tensor_tensor(v_lo[:], v_all[:, r * TPU:(r + 1) * TPU, bass.ds(g * HD, HD)],
                                   v_hi[:].bitcast(F32), ALU.subtract).then_inc(v_lo_done, 1)

            def rope_add(g, r, k):
                n = 2 * ITEMS * g + ITEMS * r + k
                b = (ITEMS * r + k) % 2
                pool.wait_ge(rope_mul, n + 1)
                if not (isinstance(g, int) and 2 * g + r == 0):
                    pool.wait_ge(scores_mm, 2 * g + r)
                else:
                    pool.wait_ge(wT_done, 1)
                dst = k_rot[:] if k == 0 else q_rot[:, k - 1, :]
                pool.tensor_tensor(dst, q_cos[b][:], q_swap[b][:], ALU.add).then_inc(rope_done, 1)

            pool.wait_ge(tok_step, 2)
            for i in (2, 3):
                select_pair(pool, i).then_inc(sel_lhs_pool, 1)
            for c in range(2 * KC):
                raw, hi, lo = ((raw_o, wo_hi, wo_lo) if c < KC else (raw_q, o_hi, o_lo))
                pool.wait_ge(wv_hi_done, c + 1)
                pool.tensor_tensor(lo[:, c % KC, :], raw[:, c % KC, :], hi[:, c % KC, :].bitcast(F32),
                                   ALU.subtract).then_inc(wv_lo_done, 1)
            qk_lo(0)
            wo_lo_split(0, range(REP))

            def group(g, first=False, last=False):
                if not first:
                    v_low(g - 1, 1)
                for k in range(ITEMS):
                    rope_add(g, 0, k)
                v_low(g, 0)
                for k in range(ITEMS):
                    rope_add(g, 1, k)
                    if not first:
                        wo_lo_split(g, (range(0, 2), range(2, 3), range(3, 4), (), ())[k])
                if not last:
                    qk_lo(g + 1)

            group(0, first=True)
            with pool.Fori(1, KV - 1) as g:
                group(g)
            group(KV - 1, last=True)
            v_low(KV - 1, 1)

        @block.scalar
        def _(act):
            act.dma_start(tok_i[:], itok.unsqueeze(0).broadcast_to([P, BATCH])).then_inc(dma_cond, 16)
            act.dma_start(wcond[:, :, 0:T], cond_v).then_inc(dma_cond, 16)
            act.dma_start(wcond[:, :, T:2 * T], cond2_v).then_inc(dma_cond, 16)
            act.dma_start(wsc[:], w_scale.broadcast_to([P, 1])).then_inc(dma_cond, 16)
            act.wait_ge(dma_const, 16)
            act.activation(ident_bf[:], ident, ACT.Copy).then_inc(const_done, 1)
            act.activation(tri_bf[:], cst[:, C_TRI:C_TRI + P], ACT.Copy).then_inc(const_done, 1)
            act.activation(pos_bf[:], cst[:, C_IDENT:C_IDENT + T].unsqueeze(1).broadcast_to([P, TPU * REP, T]),
                           ACT.Copy).then_inc(const_done, 1)

            def h_high(t):
                act.wait_ge(h_mm, t + 1)
                act.activation(hT_hi[:, :, t * P:(t + 1) * P], q_ps[t % 2][:].rearrange("p (c r) -> p c r", c=KC),
                               ACT.Copy).then_inc(h_hi_done, 1)

            def wv_high(c):
                raw, hi = (raw_o, wo_hi) if c < KC else (raw_q, o_hi)
                act.wait_ge(dma_wv, 16 if c < KC else 32)
                act.activation(hi[:, c % KC, :], raw[:, c % KC, :], ACT.Copy).then_inc(wv_hi_done, 1)

            for c in range(KC):
                wv_high(c)
            for t in range(TILES):
                h_high(t)
            for c in range(KC, 2 * KC):
                wv_high(c)
            for c in range(KC):
                act.wait_ge(dma_ffn, 16)
                if c >= 2:
                    act.wait_ge(w8_step, 3 * (c - 1))
                act.activation(tmp_scaled[c % 2], q_rot[:, c, :], ACT.Copy, scale=SHIFT).then_inc(w8_scaled, 1)

            def qk_high(g, items):
                act.wait_ge(dma_qk, 32 * (g + 1))
                for k in items:
                    if not (isinstance(g, int) and g == 0):
                        act.wait_ge(proj_mm, 2 * ITEMS * g - ITEMS + k + 1)
                    raw, hi = ((raw_k[:], wk_hi[:]) if k == 0 else
                               (w[:, :, (k - 1) * HD:k * HD] for w in (raw_q, wq_hi)))
                    act.activation(hi, raw, ACT.Copy).then_inc(qk_hi_done, 1)

            def wo_high(g, heads):
                act.wait_ge(dma_o, 16 * (g + 1))
                if isinstance(g, int) and g == 0:
                    act.wait_ge(v_mm, TILES)
                else:
                    act.wait_ge(wo_mm, 2 * TPU * g)
                for h in heads:
                    act.activation(wo_hi[:, h, :], raw_o[:, h, :], ACT.Copy).then_inc(wo_hi_done, 1)

            def swap(g, r, k):
                n = 2 * ITEMS * g + ITEMS * r + k
                b = (ITEMS * r + k) % 2
                act.wait_ge(proj_mm, n + 1)
                if not (isinstance(g, int) and 2 * g + r == 0 and k < 2):
                    act.wait_ge(rope_done, n - 1)
                ps = q_ps[ITEM_BANK[k]]
                act.activation(q_swap[b][0:P // 2, :], ps[P // 2:P, :], ACT.Copy)
                act.activation(q_swap[b][P // 2:P, :], ps[0:P // 2, :], ACT.Copy).then_inc(swap_done, 1)

            def v_high(g, r):
                u = 2 * g + r
                if not (isinstance(g, int) and u == 0):
                    act.wait_ge(pv_mm, TPU * u)
                else:
                    act.wait_ge(v_copied, 2 * TILES)
                act.activation(v_hi[:], v_all[:, r * TPU:(r + 1) * TPU, bass.ds(g * HD, HD)],
                               ACT.Copy).then_inc(v_hi_done, 1)

            def exponent(g, r):
                u = 2 * g + r
                act.wait_ge(soft_step, 7 * u + 3)
                act.activation(s_exp[:], s_nat[:], ACT.Exp, scale=SCALE).then_inc(exp_done, 1)

            def p_high(g, r):
                u = 2 * g + r
                act.wait_ge(soft_step, 7 * u + 7)
                if isinstance(g, int) and u == 0:
                    act.wait_ge(const_done, 4)
                else:
                    act.wait_ge(pv_mm, TPU * u)
                for b in range(BPT):
                    s = slice(T * b, T * b + T)
                    act.activation(pb_hi[s, :, b, :], p_tr[s, :, :], ACT.Copy).then_inc(p_hi_done, 1)

            def o_high(g, r, j):
                u = 2 * g + r
                act.wait_ge(pv_mm, TPU * u + j + 1)
                if not (isinstance(g, int) and u == 0):
                    act.wait_ge(wo_mm, TPU * u - TPU + j + 1)
                elif j == 0:
                    act.wait_ge(v_mm, 2 * TILES)
                act.activation(o_hi[:, j, :], o_ps[j % 2][:], ACT.Copy).then_inc(o_hi_done, 1)

            def softmax_and_swaps(last, cur, split_wo=None):
                if last is not None:
                    v_high(*last)
                    exponent(*last)
                if cur is not None:
                    swap(*cur, 0)
                if split_wo is not None:
                    wo_high(split_wo, range(0, 2))
                if cur is not None:
                    swap(*cur, 1)
                if split_wo is not None:
                    wo_high(split_wo, range(2, 3))
                if last is not None:
                    p_high(*last)
                if cur is not None:
                    swap(*cur, 2)
                if split_wo is not None:
                    wo_high(split_wo, range(3, 4))
                if cur is not None:
                    swap(*cur, 3)
                if last is not None:
                    o_high(*last, 0)
                    o_high(*last, 1)
                if cur is not None:
                    swap(*cur, 4)

            qk_high(0, range(ITEMS))
            wo_high(0, range(REP))

            def group(g, first=False, last=False):
                softmax_and_swaps(None if first else (g - 1, 1), (g, 0))
                if not first:
                    o_high(g - 1, 1, 2)
                    o_high(g - 1, 1, 3)
                softmax_and_swaps((g, 0), (g, 1), None if first else g)
                if not last:
                    qk_high(g + 1, range(0, 2))
                o_high(g, 0, 2)
                if not last:
                    qk_high(g + 1, range(2, 4))
                o_high(g, 0, 3)
                if not last:
                    qk_high(g + 1, range(4, 5))

            group(0, first=True)
            with act.Fori(1, KV - 1) as g:
                group(g)
            group(KV - 1, last=True)
            softmax_and_swaps((KV - 1, 1), None)
            o_high(KV - 1, 1, 2)
            o_high(KV - 1, 1, 3)

            def y_copy(t):
                act.wait_ge(y_mm, t + 1)
                if t == 0:
                    act.wait_ge(qk_lo_done, KV * ITEMS)
                    act.wait_ge(wo_lo_done, KV * REP)
                act.activation(y_t(t), q_ps[t % 3][:], ACT.Copy).then_inc(y_copied, 1)

            for t in range(TILES):
                y_copy(t)
            for t in range(TILES):
                if t == 0:
                    act.wait_ge(tail_vec, 5)
                else:
                    act.wait_ge(y8_step, 3 * (t - 1) + 1 if t < 2 else 3 * (t - 1))
                act.activation(tmp_scaled[t % 2], y_t(t), ACT.Copy, scale=col[:, 2:3]).then_inc(y_scaled, 1)
                if t >= 2:
                    act.wait_ge(y8_step, 3 * (t - 1))
                act.activation(q_swap[t % 2][:], y_t(t), ACT.Copy, scale=col[:, 1:2]).then_inc(y_scaled, 1)
            for t in range(TILES):
                act.wait_ge(tail_vec, 10)
                act.activation(v_all[:, t, 0:HID], v_all[:, t, HID:2 * HID], ACT.Copy,
                               scale=col[:, 6:7]).then_inc(f_div, 1)

        @block.tensor
        def _(pe):
            pe.wait_ge(wc_step, 5)
            for t in range(TILES):
                if t < TPU:
                    pe.wait_ge(sel_lhs, t // 2 + 1)
                else:
                    pe.wait_ge(sel_lhs_pool, t // 2 - 1)
                for k in range(4):
                    for i in range(3):
                        mm = pe.matmul(s_ps[:, t * 64:(t + 1) * 64],
                                       selector[t // 2][:, k, (t % 2) * BPT:(t % 2 + 1) * BPT, :], wc_part[i][:, k, :],
                                       start=(k == 0 and i == 0), stop=(k == 3 and i == 2))
            mm.then_inc(sel_mm, 1)
            pe.wait_ge(wbd_done, 2)
            for t in range(TILES):
                pe.wait_ge(dma_x[t // 2], 16)
                if t >= 2:
                    pe.wait_ge(h_lo_done, t - 1)
                for c in range(KC):
                    mm = pe.matmul(q_ps[t % 2][:, c * P:(c + 1) * P], xacc[:, t, c * P:(c + 1) * P],
                                   wbd1[t // TPU][:, t % TPU, :, :], start=True, stop=True)
                mm.then_inc(h_mm, 1)

            def three_pass(dst, pairs, first_wait=None):
                n = len(pairs)
                for i, ((l_hi, l_lo), (r_hi, r_lo)) in enumerate(pairs):
                    pe.matmul(dst, l_hi, r_hi, start=(i == 0), stop=False)
                    pe.matmul(dst, l_hi, r_lo, start=False, stop=False)
                    mm = pe.matmul(dst, l_lo, r_hi, start=False, stop=(i == n - 1))
                return mm

            def values(i):
                n, t = divmod(i, TILES)
                hi, lo = (wo_hi, wo_lo) if n == 0 else (o_hi, o_lo)
                if t == 0:
                    pe.wait_ge(wv_lo_done, KC * (n + 1))
                pe.wait_ge(h_lo_done, t + 1)
                if i >= 2:
                    pe.wait_ge(v_copied, i - 1)
                rows = slice(t * P, (t + 1) * P)
                three_pass(w_ps[i % 2][:], [((hT_hi[:, c, rows], hT_lo[:, c, rows]), (hi[:, c, :], lo[:, c, :]))
                                            for c in range(KC)]).then_inc(v_mm, 1)

            for i in range(2 * TILES - V_LATE):
                values(i)
            for c in range(KC):
                pe.wait_ge(w8_step, 3 * (c + 1))
                pe.wait_ge(const_done, 4)
                dst = o_ps[c // 2][:].bitcast(BF16)
                for d in range(KC):
                    mm = pe.transpose(dst[:, (c % 2) * 512 + d * P:(c % 2) * 512 + (d + 1) * P],
                                      w8(c)[:, d * P:(d + 1) * P], ident_bf[:])
                if c % 2:
                    mm.then_inc(wT_mm, 1)

            def project(g, r, items):
                u = 2 * g + r
                zero = isinstance(g, int) and u == 0
                rows = slice(r * HALF, (r + 1) * HALF)
                for k in items:
                    n = 2 * ITEMS * g + ITEMS * r + k
                    if r == 0:
                        pe.wait_ge(qk_lo_done, g * ITEMS + k + 1)
                    if not zero:
                        pe.wait_ge(rope_mul, n - 2 if k in (0, 1) else (n - 4 if k == 2 else n - 2))
                    elif k >= 3:
                        pe.wait_ge(rope_mul, n - 2)
                    w = (wk_hi, wk_lo) if k == 0 else (wq_hi, wq_lo)
                    cols = slice(0, HD) if k == 0 else slice((k - 1) * HD, k * HD)
                    three_pass(q_ps[ITEM_BANK[k]][:],
                               [((w[0][:, c, cols], w[1][:, c, cols]), (hT_hi[:, c, rows], hT_lo[:, c, rows]))
                                for c in range(KC)]).then_inc(proj_mm, 1)

            def scores(g, r):
                u = 2 * g + r
                if not (isinstance(g, int) and u == 0):
                    pe.wait_ge(soft_step, 7 * u - 6)
                else:
                    pe.wait_ge(const_done, 4)
                pe.matmul(s_ps[:], tri_bf[:], pos_bf[:], start=True, stop=False, skip_group_check=True)
                pe.wait_ge(rope_done, ITEMS * (u + 1))
                for j in range(TPU):
                    for b in range(BPT):
                        cols = slice((j * BPT + b) * T, (j * BPT + b + 1) * T)
                        mm = pe.matmul(s_ps[T * b:T * (b + 1), j * P:(j + 1) * P], k_rot[:, cols], q_rot[:, :, cols],
                                       start=False, stop=True, skip_group_check=True)
                mm.then_inc(scores_mm, 1)

            def attend(g, r, j):
                u = 2 * g + r
                if j == 0:
                    pe.wait_ge(p_lo_done, BPT * (u + 1))
                    pe.wait_ge(v_lo_done, u + 1)
                if not (isinstance(g, int) and u == 0 and j < 2):
                    pe.wait_ge(o_lo_done, TPU * u + j - 1)
                elif j == 0:
                    pe.wait_ge(wT_done, 1)
                heads = slice(j * REP, (j + 1) * REP)
                three_pass(o_ps[j % 2][:], [((v_hi[:, j, :], v_lo[:, j, :]),
                                             (pb_hi[:, heads, :, :], pb_lo[:, heads, :, :]))]).then_inc(pv_mm, 1)

            def project_out(g, r, j):
                u = 2 * g + r
                if j == 0:
                    pe.wait_ge(wo_lo_done, REP * (g + 1))
                pe.wait_ge(o_lo_done, TPU * u + j + 1)
                if not (isinstance(g, int) and u == 0 and j < 2):
                    pe.wait_ge(acc_done, TPU * u + j - 1)
                elif j == 0:
                    pe.wait_ge(v_copied, 2 * TILES)
                three_pass(w_ps[j % 2][:],
                           [((o_hi[:, j, h * P:(h + 1) * P], o_lo[:, j, h * P:(h + 1) * P]),
                             (wo_hi[:, h, :], wo_lo[:, h, :])) for h in range(REP)]).then_inc(wo_mm, 1)

            def attend_and_out(g, r, between=None):
                attend(g, r, 0)
                attend(g, r, 1)
                if between is not None:
                    project(*between, range(ITEMS - 1, ITEMS))
                for j in range(TPU):
                    project_out(g, r, j)
                    if j + 2 < TPU:
                        attend(g, r, j + 2)

            def group(g, first=False):
                project(g, 0, range(ITEMS if first else ITEMS - 1))
                if not first:
                    attend_and_out(g - 1, 1, between=(g, 0))
                else:
                    for i in range(2 * TILES - V_LATE, 2 * TILES):
                        values(i)
                scores(g, 0)
                project(g, 1, range(ITEMS - 1))
                attend_and_out(g, 0, between=(g, 1))
                scores(g, 1)

            group(0, first=True)
            with pe.Fori(1, KV) as g:
                group(g)

            def mix2(t):
                pe.wait_ge(acc_done, TPU * 2 * (KV - 1) + t + 1)
                pe.wait_ge(rope_mul, 2 * ITEMS * KV)
                if t >= 3:
                    pe.wait_ge(y_copied, t - 2)
                for c in range(KC):
                    mm = pe.matmul(q_ps[t % 3][:, c * P:(c + 1) * P], xacc[:, t, c * P:(c + 1) * P],
                                   wbd2[:, t, :, :], start=True, stop=True)
                mm.then_inc(y_mm, 1)

            for t in range(TPU - 1):
                mix2(t)
            attend_and_out(KV - 1, 1)
            for t in range(TPU - 1, TILES):
                mix2(t)

            def spread_max(n):
                pe.wait_ge(tail_vec, 5 * n + 1)
                pe.transpose(s_ps[0:1, 0:P], col[:, 4 * n:4 * n + 1], ident).then_inc(tail_mm, 1)
                pe.wait_ge(tail_vec, 5 * n + 2)
                pe.matmul(s_ps[:, P:P + 1], cst[0:1, C_ONE:C_ONE + P], row[0:1, n:n + 1],
                          start=True, stop=True).then_inc(tail_mm, 1)

            spread_max(0)
            for t in range(TILES):
                pe.wait_ge(y8_step, 3 * (t + 1))
                if t >= 2:
                    pe.wait_ge(f_done, 2 * (t - 1) - 1)
                for c in range(KC):
                    mm = pe.matmul(w_ps[t % 2][:], y8[:, t, c * P:(c + 1) * P], wT[:, c, :],
                                   start=(c == 0), stop=(c == KC - 1))
                mm.then_inc(f_mm, 1)
            spread_max(1)

        @block.vector
        def _(dve):
            dve.wait_ge(dma_cond, 64)
            dve.wait_ge(dma_const, 16)
            dve.tensor_copy(tok_f[:], tok_i[:]).then_inc(tok_step, 1)
            dve.tensor_copy(wc_part[0], wcond).then_inc(wc_step, 1)
            dve.wait_ge(tok_step, 1)
            dve.tensor_tensor(tok_eq[:], tok_f[:].unsqueeze(1).broadcast_to([P, 4, BATCH]),
                              cst[:, C_SVAL:C_SVAL + 4].unsqueeze(2).broadcast_to([P, 4, BATCH]),
                              ALU.is_equal).then_inc(tok_step, 1)
            dve.wait_ge(wc_step, 1)
            dve.tensor_tensor(wc_rest, wcond, wc_part[0], ALU.subtract).then_inc(wc_step, 1)
            for i in range(2):
                if i == 0:
                    dve.wait_ge(tok_step, 2)
                select_pair(dve, i).then_inc(sel_lhs, 1)
                if i == 0:
                    dve.wait_ge(wc_step, 2)
                    dve.tensor_copy(wc_part[1], wc_rest).then_inc(wc_step, 1)
                    dve.wait_ge(wc_step, 3)
                    dve.tensor_tensor(wc_rest, wc_rest, wc_part[1], ALU.subtract).then_inc(wc_step, 1)
                    dve.wait_ge(wc_step, 4)
                    dve.tensor_copy(wc_part[2], wc_rest).then_inc(wc_step, 1)
            dve.wait_ge(sel_mm, 1)
            picked = s_ps[:].rearrange("p (t w d) -> p t w d", w=2, d=T)
            for w, half, dst in ((0, 0, wbd1[0]), (0, 1, wbd1[1]), (1, 0, wbd2[:, 0:TPU]), (1, 1, wbd2[:, TPU:TILES])):
                src = picked[:, half * TPU:(half + 1) * TPU, w, :]
                dve.tensor_tensor(dst, src.unsqueeze(2).broadcast_to([P, TPU, BPT, T]), block_b,
                                  ALU.mult).then_inc(wbd_done, 1)

            def h_low(t):
                dve.wait_ge(h_hi_done, t + 1)
                cols = slice(t * P, (t + 1) * P)
                dve.tensor_tensor(hT_lo[:, :, cols], q_ps[t % 2][:].rearrange("p (c r) -> p c r", c=KC),
                                  hT_hi[:, :, cols].bitcast(F32), ALU.subtract).then_inc(h_lo_done, 1)

            for t in range(TILES):
                h_low(t)

            def round_e4m3(dst, scaled, plain, total, done, n):
                dve.tensor_scalar(scaled.bitcast(I32), scaled.bitcast(I32), EXP_BITS, HALF_BIT,
                                  ALU.bitwise_and, ALU.bitwise_or).then_inc(done, 1)
                dve.wait_ge(done, 3 * n + 1)
                dve.scalar_tensor_tensor(out=total, in0=scaled, scalar=LEAST, in1=plain, op0=ALU.max,
                                         op1=ALU.add).then_inc(done, 1)
                dve.wait_ge(done, 3 * n + 2)
                dve.scalar_tensor_tensor(out=dst, in0=scaled, scalar=LEAST, in1=total, op0=ALU.max,
                                         op1=ALU.subtract).then_inc(done, 1)

            def v_copy(i):
                n, t = divmod(i, TILES)
                dve.wait_ge(v_mm, i + 1)
                dve.tensor_copy(v_all[:, t, n * 512:(n + 1) * 512], w_ps[i % 2][:]).then_inc(v_copied, 1)

            for i in range(TILES):
                v_copy(i)
            for c in range(KC):
                dve.wait_ge(w8_scaled, c + 1)
                round_e4m3(w8(c), tmp_scaled[c % 2], q_rot[:, c, :], tmp_sum, w8_step, c)
                if 2 * c < TILES - V_LATE:
                    v_copy(TILES + 2 * c)
                    v_copy(TILES + 2 * c + 1)
            for h in range(2):
                dve.wait_ge(wT_mm, h + 1)
                src = o_ps[h][:].bitcast(BF16).rearrange("p (a c o) -> p a c o", a=2, c=KC)
                mm = dve.tensor_copy(wT[:, :, h * 256:(h + 1) * 256].rearrange("p c (a o) -> p a c o", a=2), src)
            mm.then_inc(wT_done, 1)

            def rope(g, r, k):
                n = 2 * ITEMS * g + ITEMS * r + k
                b = (ITEMS * r + k) % 2
                dve.wait_ge(swap_done, n + 1)
                if not (isinstance(g, int) and 2 * g + r == 0 and k < 2):
                    dve.wait_ge(rope_done, n - 1)
                dve.tensor_tensor(by_t(q_swap[b][:]), by_t(q_swap[b][:]), sin_b, ALU.mult)
                dve.tensor_tensor(by_t(q_cos[b][:]), by_t(q_ps[ITEM_BANK[k]][:]), cos_b,
                                  ALU.mult).then_inc(rope_mul, 1)

            def soft(g, r, step):
                u = 2 * g + r
                if step == 0:
                    dve.wait_ge(scores_mm, u + 1)
                elif step != 3:
                    dve.wait_ge(soft_step, 7 * u + step)
                if step == 0:
                    op = dve.transpose(s_nat[:].rearrange("p a t -> p (a t)"), s_ps[:])
                elif step == 1:
                    op = dve.tensor_reduce(s_max[:], s_nat[:], AX_X, ALU.max)
                elif step == 2:
                    op = dve.tensor_tensor(s_nat[:], s_nat[:], s_max[:].unsqueeze(2).broadcast_to([P, TPU * REP, T]),
                                           ALU.subtract)
                elif step == 3:
                    dve.wait_ge(exp_done, u + 1)
                    op = dve.tensor_reduce(s_sum[:], s_exp[:], AX_X, ALU.add)
                elif step == 4:
                    op = dve.reciprocal(s_rec[:], s_sum[:])
                elif step == 5:
                    op = dve.tensor_tensor(s_nat[:], s_exp[:], s_rec[:].unsqueeze(2).broadcast_to([P, TPU * REP, T]),
                                           ALU.mult)
                elif step == 6:
                    if not (isinstance(g, int) and u == 0):
                        dve.wait_ge(p_hi_done, BPT * u)
                    op = dve.transpose(p_tr[:].rearrange("p a t -> p (a t)"), s_nat[:].rearrange("p a t -> p (a t)"))
                op.then_inc(soft_step, 1)

            def p_low(g, r):
                u = 2 * g + r
                for b in range(BPT):
                    s = slice(T * b, T * b + T)
                    dve.wait_ge(p_hi_done, BPT * u + b + 1)
                    if b == 0 and not (isinstance(g, int) and u == 0):
                        dve.wait_ge(pv_mm, TPU * u)
                    dve.tensor_tensor(pb_lo[s, :, b, :], p_tr[s, :, :], pb_hi[s, :, b, :].bitcast(F32),
                                      ALU.subtract).then_inc(p_lo_done, 1)

            def o_low(g, r, j):
                u = 2 * g + r
                dve.wait_ge(o_hi_done, TPU * u + j + 1)
                dve.tensor_tensor(o_lo[:, j, :], o_ps[j % 2][:], o_hi[:, j, :].bitcast(F32),
                                  ALU.subtract).then_inc(o_lo_done, 1)

            def accumulate(g, r, j):
                u = 2 * g + r
                tile = r * TPU + j
                dve.wait_ge(wo_mm, TPU * u + j + 1)
                if not (isinstance(g, int) and g == 0):
                    dve.wait_ge(acc_done, TPU * u - TPU)
                dve.tensor_tensor(xacc[:, tile, :], xacc[:, tile, :], w_ps[j % 2][:], ALU.add).then_inc(acc_done, 1)

            def softmax_and_ropes(last, cur):
                if last is not None:
                    soft(*last, 0)
                    soft(*last, 1)
                    soft(*last, 2)
                if cur is not None:
                    rope(*cur, 0)
                if last is not None:
                    for step in range(3, 7):
                        soft(*last, step)
                if cur is not None:
                    rope(*cur, 1)
                if last is not None:
                    p_low(*last)
                if cur is not None:
                    rope(*cur, 2)
                if last is not None:
                    o_low(*last, 0)
                    o_low(*last, 1)
                if cur is not None:
                    rope(*cur, 3)
                    rope(*cur, 4)

            def outputs(last):
                for j in range(TPU):
                    accumulate(*last, j)
                    if j + 2 < TPU:
                        o_low(*last, j + 2)

            def group(g, first=False):
                softmax_and_ropes(None if first else (g - 1, 1), (g, 0))
                if not first:
                    outputs((g - 1, 1))
                else:
                    for i in range(2 * TILES - V_LATE, 2 * TILES):
                        v_copy(i)
                softmax_and_ropes((g, 0), (g, 1))
                outputs((g, 0))

            group(0, first=True)
            with dve.Fori(1, KV) as g:
                group(g)
            softmax_and_ropes((KV - 1, 1), None)
            outputs((KV - 1, 1))

            for t in range(TILES):
                dve.wait_ge(y_copied, t + 1)
                dve.tensor_reduce(y_max[:, t:t + 1], y_t(t), AX_X, ALU.max,
                                  apply_absolute_value=True).then_inc(y_amax, 1)

            def amax_steps(n, per_tile, ready, count):
                dve.wait_ge(ready, count)
                dve.tensor_reduce(col[:, 4 * n:4 * n + 1], per_tile[:], AX_X, ALU.max).then_inc(tail_vec, 1)
                dve.wait_ge(tail_mm, 2 * n + 1)
                dve.tensor_reduce(row[0:1, n:n + 1], s_ps[0:1, 0:P], AX_X, ALU.max).then_inc(tail_vec, 1)
                dve.wait_ge(tail_mm, 2 * n + 2)
                dve.tensor_scalar(col[:, 4 * n + 3:4 * n + 4], s_ps[:, P:P + 1], 1e-12, 1.0 / FP8_MAX, ALU.max,
                                  ALU.mult).then_inc(tail_vec, 1)

            amax_steps(0, y_max, y_amax, TILES)
            dve.wait_ge(tail_vec, 3)
            dve.reciprocal(col[:, 1:2], col[:, 3:4]).then_inc(tail_vec, 1)
            dve.tensor_scalar(col[:, 8:9], col[:, 3:4], wsc[:, 0:1], None, ALU.mult)
            dve.wait_ge(tail_vec, 4)
            dve.tensor_scalar(col[:, 2:3], col[:, 1:2], SHIFT, None, ALU.mult).then_inc(tail_vec, 1)

            dve.wait_ge(dma_ffn, 32)

            def f_take(t):
                dve.wait_ge(f_mm, t + 1)
                f = v_all[:, t, HID:2 * HID]
                dve.scalar_tensor_tensor(out=f, in0=w_ps[t % 2][:], scalar=col[:, 8:9], in1=bias_b,
                                         op0=ALU.mult, op1=ALU.add).then_inc(f_done, 1)
                dve.wait_ge(f_done, 2 * t + 1)
                dve.tensor_reduce(f_max[:, t:t + 1], f, AX_X, ALU.max,
                                  apply_absolute_value=True).then_inc(f_done, 1)

            for t in range(TILES):
                dve.wait_ge(y_scaled, 2 * (t + 1))
                round_e4m3(y8[:, t, :], tmp_scaled[t % 2], q_swap[t % 2][:], tmp_sum, y8_step, t)
                if t >= 1:
                    f_take(t - 1)
            f_take(TILES - 1)
            amax_steps(1, f_max, f_done, 2 * TILES)
            dve.wait_ge(tail_vec, 8)
            dve.reciprocal(col[:, 6:7], col[:, 7:8]).then_inc(tail_vec, 1)
            dve.wait_ge(tail_vec, 9)
            dve.tensor_copy(col[:, 9:10], col[:, 7:8]).then_inc(tail_vec, 1)
            dve.wait_ge(tail_vec, 10)
            for t in range(TILES):
                f = v_all[:, t, 0:HID]
                dve.wait_ge(f_div, t + 1)
                dve.tensor_scalar(f, f, FP8_MAX, -FP8_MAX, ALU.min, ALU.max).then_inc(f_clip, 1)
                dve.wait_ge(f_clip, t + 1)
                dve.scalar_tensor_tensor(out=xacc[:, t, :], in0=f, scalar=col[:, 9:10], in1=xacc[:, t, :],
                                         op0=ALU.mult, op1=ALU.add).then_inc(result, 1)


_INS = ["x", "itok_B_0_15", "L0_cond_weights", "L0_attn_wq", "L0_attn_wk", "L0_attn_wv", "L0_attn_wo",
        "L0_cond2_weights", "L0_ffn_qweight", "L0_ffn_weight_scale", "L0_ffn_bias"]


def kernel(**inputs):
    import concourse.bacc as bacc
    from concourse.bass_utils import run_bass_kernel_spmd

    nc = bacc.Bacc("TRN2", target_bir_lowering=False, num_devices=1)
    arrays, args = {}, []
    for name in _INS:
        a = np.ascontiguousarray(inputs[name])
        if a.ndim == 0:
            a = a.reshape(1)
        arrays[f"in_{name}"] = a
    arrays["in_constants"] = constant_table()
    for name, a in arrays.items():
        args.append(nc.dram_tensor(name, a.shape, mybir.dt.from_np(a.dtype), kind="ExternalInput").ap())
    out = nc.dram_tensor("out_0", (BATCH, T, HID), F32, kind="ExternalOutput").ap()
    build(nc, *args, out)
    r = run_bass_kernel_spmd(nc, [arrays], core_ids=[0])
    return r.results[0]["out_0"]
```

```python
from contextlib import ExitStack

import numpy as np

import concourse.bass as bass
from concourse import mybir

F32 = mybir.dt.float32
F32R = mybir.dt.float32r
BF16 = mybir.dt.bfloat16
I32 = mybir.dt.int32
ALU = mybir.AluOpType
ACT = mybir.ActivationFunctionType
AX_X = mybir.AxisListType.X

P = 128
BATCH, T, HID = 32, 32, 512
HEADS, KV, HD = 32, 8, 128
CONDS = 16
REP = HEADS // KV
ROWS = BATCH * T
TILES = ROWS // P
BPT = P // T
KC = HID // P
HALF = ROWS // 2
TPU = TILES // 2
BPU = HALF // T
ITEMS = 1 + REP
SCALE = 1.0 / float(np.sqrt(HD))
MASKED = -1.0e30
FP8_MAX = 448.0
EXP_BITS = 0x7F800000
HALF_BIT = 0x00400000
SHIFT = float(2 ** 20)
LEAST = 1.5 * 2.0 ** 14

C_COS, C_SIN, C_SVAL, C_CSEL, C_BLOCK, C_IDENT, C_TRI, C_ONE = 0, 32, 64, 68, 100, 104, 232, 264
C_WIDTH = C_ONE + P
V_LATE = 4
BY_POOL = (1, 3)
BIAS_ROWS = 33
SOFT_STEPS = 8
ITEM_BANK = [0, 1, 2, 0, 1]


def constant_table():
    theta, factor, hi_ff, lo_ff, orig_max = 500000.0, 8.0, 4.0, 1.0, 1024
    inv = 1.0 / theta ** (np.arange(0, HD, 2, dtype=np.float64) / HD)
    wavelen = 2.0 * np.pi / inv
    low_wl, high_wl = orig_max / lo_ff, orig_max / hi_ff
    smooth = (orig_max / wavelen - lo_ff) / (hi_ff - lo_ff)
    scaled = np.where(wavelen > low_wl, inv / factor, inv)
    mid = (wavelen <= low_wl) & (wavelen >= high_wl)
    scaled = np.where(mid, (1 - smooth) * inv / factor + smooth * inv, scaled).astype(np.float32)
    freqs = np.arange(T, dtype=np.float32)[:, None] * scaled[None, :]
    emb = np.concatenate([freqs, freqs], axis=-1)
    sign = np.where(np.arange(HD) < HD // 2, -1.0, 1.0).astype(np.float32)
    part = np.arange(P)
    table = np.zeros((P, C_WIDTH), np.float32)
    table[:, C_COS:C_COS + T] = np.cos(emb).T
    table[:, C_SIN:C_SIN + T] = np.sin(emb).T * sign[:, None]
    table[:, C_SVAL:C_SVAL + 4] = (P // T) * np.arange(4)[None, :] + part[:, None] // T
    table[:, C_CSEL:C_CSEL + T] = part[:, None] % T == np.arange(T)[None, :]
    table[:, C_BLOCK:C_BLOCK + 4] = part[:, None] // T == np.arange(4)[None, :]
    table[:, C_IDENT:C_IDENT + P] = np.eye(P)
    table[:, C_TRI:C_TRI + T] = np.where(np.arange(T)[None, :] > part[:, None] % T, MASKED, 0.0)
    table[0, C_ONE:C_ONE + P] = 1.0
    return table


def build(nc, x, itok, cond_w, wq, wk, wv, wo, cond2_w, qweight, w_scale, bias, consts, out):
    with ExitStack() as ctx:
        def sb(name, shape, dt=F32):
            return ctx.enter_context(nc.sbuf_tensor(name, shape, dt))

        def sem(name):
            return ctx.enter_context(nc.semaphore(name))

        cst = sb("cst", [P, C_WIDTH])
        ident_bf = sb("ident_bf", [P, P], BF16)
        xacc = sb("xacc", [P, TILES, HID])
        hT_hi = sb("hT_hi", [P, KC, ROWS], F32R)
        hT_lo = sb("hT_lo", [P, KC, ROWS], F32R)
        v_all = sb("v_all", [P, TILES, KV * HD])
        wq_hi = sb("wq_hi", [P, KC, REP * HD], F32R)
        wq_lo = sb("wq_lo", [P, KC, REP * HD], F32R)
        wk_hi = sb("wk_hi", [P, KC, HD], F32R)
        wk_lo = sb("wk_lo", [P, KC, HD], F32R)
        wo_hi = sb("wo_hi", [P, REP, HID], F32R)
        wo_lo = sb("wo_lo", [P, REP, HID], F32R)
        raw_q = sb("raw_q", [P, KC, REP * HD])
        raw_k = sb("raw_k", [P, KC, HD])
        raw_o = sb("raw_o", [P, REP, HID])
        o_hi = sb("o_hi", [P, TPU, REP * P], F32R)
        o_lo = sb("o_lo", [P, TPU, REP * P], F32R)
        q_rot = sb("q_rot", [P, REP, HALF])
        k_rot = sb("k_rot", [P, HALF])
        q_cos = [sb(f"q_cos{i}", [P, HALF]) for i in range(2)]
        q_swap = [sb(f"q_swap{i}", [P, HALF]) for i in range(2)]
        s_nat = sb("s_nat", [P, TPU * REP, T])
        s_exp = sb("s_exp", [P, TPU * REP, T])
        p_tr = sb("p_tr", [P, TPU * REP, T])
        s_max = sb("s_max", [P, TPU * REP])
        s_sum = sb("s_sum", [P, TPU * REP])
        s_rec = sb("s_rec", [P, TPU * REP])
        p_st = [sb(f"p_st{i}", [P, TPU * REP, 2, T], F32R) for i in range(2)]
        v_st = [sb(f"v_st{i}", [P, TPU, HD], F32R) for i in range(2)]
        v_lo = [sb(f"v_lo{i}", [P, TPU, HD], F32R) for i in range(2)]
        wbd2 = sb("wbd2", [P, TILES, BPT, T])
        tok_i = sb("tok_i", [P, BATCH], I32)
        tok_f = sb("tok_f", [P, BATCH])
        tok_eq = sb("tok_eq", [P, 4, BATCH])
        w8 = sb("w8", [P, KC, HID], BF16)
        wsc = sb("wsc", [P, 1])
        y_max = sb("y_max", [P, TILES])
        f_max = sb("f_max", [P, TILES])
        col = sb("col", [P, 12])
        row = sb("row", [1, 4])
        ones_r = sb("ones_r", [BIAS_ROWS, P], F32R)

        bank = [ctx.enter_context(nc.psum_tensor(f"bank{i}", [P, 512], F32)) for i in range(8)]
        q_ps = bank[0:3]
        s_ps = bank[3]
        o_ps = bank[4:6]
        w_ps = bank[6:8]
        sel_ps = [s_ps, o_ps[0]]

        dma_const, dma_x, dma_cond, dma_wv, dma_ffn = (sem(n) for n in ("dma_const", "dma_x0", "dma_cond", "dma_wv", "dma_ffn"))
        dma_x = [dma_x] + [sem(f"dma_x{i}") for i in range(1, TILES // 2)]
        dma_qk, dma_o, dma_out = sem("dma_qk"), sem("dma_o"), sem("dma_out")
        const_done, ones_zeroed, warm_done = sem("const_done"), sem("ones_zeroed"), sem("warm_done")
        tok_step, wc_step, sel_lhs, sel_lhs_pool = sem("tok_step"), sem("wc_step"), sem("sel_lhs"), sem("sel_lhs_pool")
        sel_mm, wbd_done = sem("sel_mm"), sem("wbd_done")
        h_mm, h_hi_done, h_lo_done = sem("h_mm"), sem("h_hi_done"), sem("h_lo_done")
        wv_hi_done, wv_lo_done, v_mm, v_copied = sem("wv_hi_done"), sem("wv_lo_done"), sem("v_mm"), sem("v_copied")
        w8_scaled, w8_step, wT_mm, wT_done = sem("w8_scaled"), sem("w8_step"), sem("wT_mm"), sem("wT_done")
        qk_hi_done, qk_lo_done, wo_hi_done, wo_lo_done = (sem(n) for n in ("qk_hi_done", "qk_lo_done", "wo_hi_done", "wo_lo_done"))
        proj_mm, swap_done, rope_mul, rope_done = sem("proj_mm"), sem("swap_done"), sem("rope_mul"), sem("rope_done")
        scores_mm, soft_step, exp_done = sem("scores_mm"), sem("soft_step"), sem("exp_done")
        p_hi_done, p_lo_done, v_hi_done, v_lo_done = (sem(n) for n in ("p_hi_done", "p_lo_done", "v_hi_done", "v_lo_done"))
        pv_mm, o_hi_done, o_lo_done, wo_mm, acc_done = (sem(n) for n in ("pv_mm", "o_hi_done", "o_lo_done", "wo_mm", "acc_done"))
        y_mm, y_copied, y_amax, tail_mm, tail_vec = (sem(n) for n in ("y_mm", "y_copied", "y_amax", "tail_mm", "tail_vec"))
        y_div_done, y_exp_done, y8_magic, y8_sum, y8_done = (
            sem(n) for n in ("y_div_done", "y_exp_done", "y8_magic", "y8_sum", "y8_done"))
        bias_step, bias_done, bias_hi_done = (sem(n) for n in ("bias_step", "bias_done", "bias_hi_done"))
        f_mm, f_amax, f_kept, f_step, f_div_done, f_clip, f_back, result, result_pool = (
            sem(n) for n in ("f_mm", "f_amax", "f_kept", "f_step", "f_div_done", "f_clip", "f_back", "result", "result_pool"))

        x_rows = x.rearrange("(j b) c h -> j (b c) h", b=BPT)
        out_rows = out.rearrange("(j b) c h -> j (b c) h", b=BPT)
        wq_v = wq.rearrange("(c p) n -> p c n", p=P)
        wk_v = wk.rearrange("(c p) n -> p c n", p=P)
        wv_v = wv.rearrange("(c p) n -> p c n", p=P)
        wo_v = wo.rearrange("(h p) n -> p h n", p=P)
        qw_v = qweight.rearrange("(c p) n -> p c n", p=P)
        cond_v = cond_w.rearrange("(k s) c d -> (s c) k d", k=4)
        cond2_v = cond2_w.rearrange("(k s) c d -> (s c) k d", k=4)
        cos_b = cst[:, C_COS:C_COS + T].unsqueeze(1).broadcast_to([P, BPU, T])
        sin_b = cst[:, C_SIN:C_SIN + T].unsqueeze(1).broadcast_to([P, BPU, T])
        ident = cst[:, C_IDENT:C_IDENT + P]
        mask_b = cst[:, C_TRI:C_TRI + T].unsqueeze(1).broadcast_to([P, TPU * REP, T])
        csel_b = cst[:, C_CSEL:C_CSEL + T].unsqueeze(1).unsqueeze(1).broadcast_to([P, 4, 2 * BPT, T])
        block_b = cst[:, C_BLOCK:C_BLOCK + BPT].unsqueeze(1).unsqueeze(3).broadcast_to([P, TPU, BPT, T])
        flat = lambda a: a[:].rearrange("p a t -> p (a t)")
        selector = [a.bitcast(BF16).rearrange("p (k b c) -> p k b c", k=4, c=T)
                    for a in (q_cos[0][:], q_cos[1][:], flat(s_nat), flat(s_exp))]
        wc_rest = k_rot[:, 256:512].rearrange("p (k n) -> p k n", k=4)
        wc_part = [flat(p_tr).bitcast(BF16)[:, i * 256:(i + 1) * 256].rearrange("p (k n) -> p k n", k=4)
                   for i in range(3)]
        warm = w8[:, 0, :]
        wbd1 = [a[:].rearrange("p (t b d) -> p t b d", t=TPU, b=BPT) for a in q_swap]
        wcond = k_rot[:, 0:4 * 2 * T].rearrange("p (k n) -> p k n", k=4)
        wT = [a[:].bitcast(BF16).rearrange("p (c o) -> p c o", c=KC // 2) for a in q_cos]
        y8 = q_rot[:].bitcast(BF16).rearrange("p h (a n) -> p (h a) n", a=2)
        bias_row = raw_k[0:BIAS_ROWS].rearrange("p c n -> p (c n)")
        bias_sc = k_rot[0:BIAS_ROWS, :]
        bias_parts = wk_hi[0:BIAS_ROWS].rearrange("p c n -> p (c n)")
        y_div = lambda t: v_all[:, t, 0:HID]
        y_exp = lambda t: v_all[:, t, HID:2 * HID]
        f_div = lambda t: v_all[:, t, HID:2 * HID]
        f_keep = v_all[:, 0, 0:HID]
        by_t = lambda a: a.rearrange("p (b t) -> p b t", t=T)
        y_t = lambda t: (raw_q if t < TPU else raw_o)[:, t % TPU, :]
        y_sum = [flat(p_tr), flat(s_nat)]
        tmp_scaled = [s_nat[:].rearrange("p a t -> p (a t)"), s_exp[:].rearrange("p a t -> p (a t)")]
        tmp_sum = p_tr[:].rearrange("p a t -> p (a t)")

        def select_pair(eng, i):
            eq_b = tok_eq[:, :, 2 * i * BPT:2 * (i + 1) * BPT].unsqueeze(3).broadcast_to([P, 4, 2 * BPT, T])
            return eng.tensor_tensor(selector[i], eq_b, csel_b, ALU.mult)

        block = ctx.enter_context(nc.Block())

        @block.sync
        def _(sp):
            sp.dma_start(tok_i[:], itok.unsqueeze(0).broadcast_to([P, BATCH])).then_inc(dma_cond, 16)
            sp.dma_start(wcond[:, :, 0:T], cond_v).then_inc(dma_cond, 16)
            sp.dma_start(wcond[:, :, T:2 * T], cond2_v).then_inc(dma_cond, 16)
            sp.dma_start(cst[:], consts).then_inc(dma_const, 16)
            sp.dma_start(wsc[:], w_scale.broadcast_to([P, 1])).then_inc(dma_cond, 16)
            for t in range(0, TILES, 2):
                sp.dma_start(xacc[:, t:t + 2, :], x_rows[t:t + 2].rearrange("t p h -> p t h")).then_inc(dma_x[t // 2], 16)
                if t == 0:
                    sp.dma_start(raw_o[:], wv_v[:, :, 0:512]).then_inc(dma_wv, 16)
            sp.wait_ge(dma_wv, 16)
            sp.dma_start(raw_q[:], wv_v[:, :, 512:1024]).then_inc(dma_wv, 16)
            sp.dma_start(raw_k[:], wk_v[:, :, 0:HD]).then_inc(dma_qk, 16)
            sp.dma_start(q_rot[:], qw_v).then_inc(dma_ffn, 16)

            def load_weights(g):
                if isinstance(g, int) and g == 0:
                    sp.wait_ge(wv_lo_done, 2 * KC)
                else:
                    sp.wait_ge(qk_lo_done, g * ITEMS)
                    sp.dma_start(raw_k[:], wk_v[:, :, bass.ds(g * HD, HD)]).then_inc(dma_qk, 16)
                sp.dma_start(raw_q[:], wq_v[:, :, bass.ds(g * REP * HD, REP * HD)]).then_inc(dma_qk, 16)
                if not (isinstance(g, int) and g == 0):
                    sp.wait_ge(wo_lo_done, g * REP)
                sp.dma_start(raw_o[:], wo_v[:, bass.ds(g * REP, REP), :]).then_inc(dma_o, 16)

            load_weights(0)
            with sp.Fori(1, KV) as g:
                load_weights(g)
            sp.wait_ge(qk_lo_done, KV * ITEMS)
            sp.dma_start(bias_row, bias.unsqueeze(0).broadcast_to([BIAS_ROWS, HID])).then_inc(dma_ffn, 16)
            for t in range(TILES):
                if t in BY_POOL:
                    sp.wait_ge(result_pool, BY_POOL.index(t) + 1)
                else:
                    sp.wait_ge(result, t + 1 - sum(p < t for p in BY_POOL))
                sp.dma_start(out_rows[t], xacc[:, t, :]).then_inc(dma_out, 16)
            sp.wait_ge(dma_out, 16 * TILES)

        @block.gpsimd
        def _(pool):
            pool.memset(p_st[0][:].bitcast(F32), 0.0)
            pool.memset(v_lo[0][:].bitcast(F32), 0.0)
            pool.memset(v_lo[1][:].bitcast(F32), 0.0)
            pool.memset(p_st[1][:].bitcast(F32), 0.0).then_inc(const_done, 1)

            def qk_lo(g):
                for k in range(ITEMS):
                    pool.wait_ge(qk_hi_done, g * ITEMS + k + 1)
                    raw, hi, lo = ((raw_k[:], wk_hi[:], wk_lo[:]) if k == 0 else
                                   (w[:, :, (k - 1) * HD:k * HD] for w in (raw_q, wq_hi, wq_lo)))
                    pool.tensor_tensor(lo, raw, hi.bitcast(F32), ALU.subtract).then_inc(qk_lo_done, 1)

            def wo_lo_split(g, heads):
                for h in heads:
                    pool.wait_ge(wo_hi_done, g * REP + h + 1)
                    pool.tensor_tensor(wo_lo[:, h, :], raw_o[:, h, :], wo_hi[:, h, :].bitcast(F32),
                                       ALU.subtract).then_inc(wo_lo_done, 1)

            def v_low(g, r):
                u = 2 * g + r
                if isinstance(g, int) and u == 0:
                    pool.wait_ge(const_done, 2)
                pool.wait_ge(v_hi_done, u + 1)
                for i in range(2):
                    own = slice(64 * i, 64 * (i + 1))
                    pool.tensor_tensor(v_lo[i][own], v_all[own, r * TPU:(r + 1) * TPU, bass.ds(g * HD, HD)],
                                       v_st[i][own].bitcast(F32), ALU.subtract).then_inc(v_lo_done, 1)
                pool.wait_ge(v_lo_done, 2 * (u + 1))

            def rope_add(g, r, k):
                n = 2 * ITEMS * g + ITEMS * r + k
                b = (ITEMS * r + k) % 2
                pool.wait_ge(rope_mul, n + 1)
                if not (isinstance(g, int) and 2 * g + r == 0):
                    pool.wait_ge(scores_mm, 2 * g + r)
                else:
                    pool.wait_ge(w8_step, 3 * KC)
                dst = k_rot[:] if k == 0 else q_rot[:, k - 1, :]
                pool.tensor_tensor(dst, q_cos[b][:], q_swap[b][:], ALU.add).then_inc(rope_done, 1)

            pool.wait_ge(tok_step, 2)
            for i in (1, 3):
                select_pair(pool, i).then_inc(sel_lhs_pool, 1)
            for c in range(2 * KC):
                raw, hi, lo = ((raw_o, wo_hi, wo_lo) if c < KC else (raw_q, o_hi, o_lo))
                pool.wait_ge(wv_hi_done, c + 1)
                pool.tensor_tensor(lo[:, c % KC, :], raw[:, c % KC, :], hi[:, c % KC, :].bitcast(F32),
                                   ALU.subtract).then_inc(wv_lo_done, 1)
            qk_lo(0)
            wo_lo_split(0, range(REP))

            def stage(cur, split_wo=None, split_qk=None):
                if split_wo is not None:
                    wo_lo_split(split_wo, range(0, 2))
                rope_add(*cur, 0)
                if split_wo is not None:
                    wo_lo_split(split_wo, range(2, 4))
                for k in range(1, ITEMS):
                    rope_add(*cur, k)
                if split_qk is not None:
                    qk_lo(split_qk)
                    pool.wait_ge(qk_lo_done, (split_qk + 1) * ITEMS)
                else:
                    pool.wait_ge(rope_done, ITEMS * (2 * cur[0] + cur[1] + 1))
                v_low(*cur)

            stage((0, 0))
            stage((0, 1), split_qk=1)
            with pool.Fori(1, KV - 1) as g:
                stage((g, 0))
                stage((g, 1), split_wo=g, split_qk=g + 1)
            stage((KV - 1, 0))
            stage((KV - 1, 1), split_wo=KV - 1)
            for i, t in enumerate(BY_POOL):
                pool.wait_ge(f_back, i + 1)
                pool.tensor_tensor(xacc[:, t, :], f_div(t), xacc[:, t, :], ALU.add).then_inc(result_pool, 1)

        @block.scalar
        def _(act):
            act.wait_ge(dma_cond, 64)
            act.activation(wc_part[0], wcond, ACT.Copy).then_inc(wc_step, 1)
            for i in (1, 2):
                act.wait_ge(wc_step, 2 * i)
                act.activation(wc_part[i], wc_rest, ACT.Copy).then_inc(wc_step, 1)
            act.wait_ge(dma_const, 16)
            act.activation(ident_bf[:], ident, ACT.Copy).then_inc(const_done, 1)

            def h_high(t):
                act.wait_ge(h_mm, t + 1)
                act.activation(hT_hi[:, :, t * P:(t + 1) * P], q_ps[t % 3][:].rearrange("p (c r) -> p c r", c=KC),
                               ACT.Copy).then_inc(h_hi_done, 1)

            def wv_high(c):
                raw, hi = (raw_o, wo_hi) if c < KC else (raw_q, o_hi)
                act.wait_ge(dma_wv, 16 if c < KC else 32)
                act.activation(hi[:, c % KC, :], raw[:, c % KC, :], ACT.Copy).then_inc(wv_hi_done, 1)

            for c in range(KC):
                wv_high(c)
            for t in range(TILES):
                h_high(t)
            for c in range(KC, 2 * KC):
                wv_high(c)
            for c in range(KC):
                act.wait_ge(dma_ffn, 16)
                if c >= 2:
                    act.wait_ge(w8_step, 3 * (c - 1))
                act.activation(tmp_scaled[c % 2], q_rot[:, c, :], ACT.Copy, scale=SHIFT).then_inc(w8_scaled, 1)

            def qk_high(g, items):
                act.wait_ge(dma_qk, 32 * (g + 1))
                for k in items:
                    if not (isinstance(g, int) and g == 0):
                        act.wait_ge(proj_mm, 2 * ITEMS * g - ITEMS + k + 1)
                    raw, hi = ((raw_k[:], wk_hi[:]) if k == 0 else
                               (w[:, :, (k - 1) * HD:k * HD] for w in (raw_q, wq_hi)))
                    act.activation(hi, raw, ACT.Copy).then_inc(qk_hi_done, 1)

            def wo_high(g, heads):
                act.wait_ge(dma_o, 16 * (g + 1))
                if isinstance(g, int) and g == 0:
                    act.wait_ge(v_mm, TILES)
                else:
                    act.wait_ge(wo_mm, 2 * TPU * g)
                for h in heads:
                    act.activation(wo_hi[:, h, :], raw_o[:, h, :], ACT.Copy).then_inc(wo_hi_done, 1)

            def swap(g, r, k):
                n = 2 * ITEMS * g + ITEMS * r + k
                b = (ITEMS * r + k) % 2
                act.wait_ge(proj_mm, n + 1)
                if not (isinstance(g, int) and 2 * g + r == 0 and k < 2):
                    act.wait_ge(rope_done, n - 1)
                ps = q_ps[ITEM_BANK[k]]
                act.activation(q_swap[b][0:P // 2, :], ps[P // 2:P, :], ACT.Copy)
                act.activation(q_swap[b][P // 2:P, :], ps[0:P // 2, :], ACT.Copy).then_inc(swap_done, 1)

            def v_high(g, r):
                u = 2 * g + r
                if not (isinstance(g, int) and u == 0):
                    act.wait_ge(pv_mm, TPU * u)
                else:
                    act.wait_ge(v_copied, 2 * TILES)
                for i in range(2):
                    for half in range(2):
                        op = act.activation(v_st[i][64 * half:64 * (half + 1)],
                                            v_all[64 * i:64 * (i + 1), r * TPU:(r + 1) * TPU, bass.ds(g * HD, HD)],
                                            ACT.Copy)
                op.then_inc(v_hi_done, 1)

            def exponent(g, r):
                u = 2 * g + r
                act.wait_ge(soft_step, SOFT_STEPS * u + 4)
                act.activation(s_exp[:], s_nat[:], ACT.Exp, scale=SCALE).then_inc(exp_done, 1)

            def p_high(g, r):
                u = 2 * g + r
                act.wait_ge(soft_step, SOFT_STEPS * (u + 1))
                if isinstance(g, int) and u == 0:
                    act.wait_ge(const_done, 2)
                else:
                    act.wait_ge(pv_mm, TPU * u)
                for b in range(BPT):
                    s = slice(T * b, T * b + T)
                    act.activation(p_st[b // 2][s, :, b % 2, :], p_tr[s, :, :], ACT.Copy).then_inc(p_hi_done, 1)

            def o_high(g, r, j):
                u = 2 * g + r
                act.wait_ge(pv_mm, TPU * u + j + 1)
                if not (isinstance(g, int) and u == 0):
                    act.wait_ge(wo_mm, TPU * u - TPU + j + 1)
                elif j == 0:
                    act.wait_ge(v_mm, 2 * TILES)
                act.activation(o_hi[:, j, :], o_ps[j % 2][:], ACT.Copy).then_inc(o_hi_done, 1)

            qk_high(0, range(ITEMS))
            wo_high(0, range(REP))

            def stage(cur, last, split_wo=None, split_qk=None, early_scores=False):
                if split_wo is not None:
                    wo_high(split_wo, range(0, 2))
                swap(*cur, 0)
                if split_wo is not None:
                    wo_high(split_wo, range(2, 4))
                swap(*cur, 1)
                swap(*cur, 2)
                if last is not None:
                    o_high(*last, 0)
                swap(*cur, 3)
                if last is not None:
                    o_high(*last, 1)
                swap(*cur, 4)
                if split_qk is not None:
                    qk_high(split_qk, range(0, 2))
                if last is not None:
                    o_high(*last, 2)
                if split_qk is not None:
                    qk_high(split_qk, range(2, 4))
                if last is not None and not early_scores:
                    o_high(*last, 3)
                if split_qk is not None:
                    qk_high(split_qk, range(4, 5))
                if last is not None and not early_scores:
                    v_high(*cur)
                exponent(*cur)
                if early_scores:
                    o_high(*last, 3)
                    v_high(*cur)
                p_high(*cur)
                if last is None:
                    v_high(*cur)

            stage((0, 0), None)
            stage((0, 1), (0, 0), split_qk=1)
            with act.Fori(1, KV - 1) as g:
                stage((g, 0), (g - 1, 1))
                stage((g, 1), (g, 0), split_wo=g, split_qk=g + 1)
            stage((KV - 1, 0), (KV - 2, 1))
            stage((KV - 1, 1), (KV - 1, 0), split_wo=KV - 1, early_scores=True)

            def y_copy(t):
                act.wait_ge(y_mm, t + 1)
                if t == 0:
                    act.wait_ge(qk_lo_done, KV * ITEMS)
                    act.wait_ge(wo_lo_done, KV * REP)
                if t >= TILES - 2:
                    act.wait_ge(y_amax, t + 1)
                act.activation(y_t(t), q_ps[t % 3][:], ACT.Copy).then_inc(y_copied, 1)

            last = (KV - 1, 1)
            for t in range(TPU - 1):
                y_copy(t)
            o_high(*last, 0)
            o_high(*last, 1)
            y_copy(TPU - 1)
            o_high(*last, 2)
            y_copy(TPU)
            o_high(*last, 3)
            y_copy(TPU + 1)
            y_copy(TPU + 2)
            for h in range(2):
                act.wait_ge(wT_mm, h + 1)
                src = o_ps[h][:].bitcast(BF16).rearrange("p (a c o) -> p a c o", a=2, c=KC)
                for i in range(2):
                    dst = wT[i][:, :, 2 * h * P:2 * (h + 1) * P].rearrange("p c (a o) -> p a c o", a=2)
                    act.activation(dst, src[:, :, 2 * i:2 * (i + 1), :], ACT.Copy).then_inc(wT_done, 1)
            y_copy(TPU + 3)
            for t in range(TILES):
                if t == 0:
                    act.wait_ge(tail_vec, 4)
                act.activation(y_div(t), y_t(t), ACT.Copy, scale=col[:, 1:2]).then_inc(y_div_done, 1)
                if t == 1:
                    act.wait_ge(tail_vec, 5)
                if t > 0:
                    act.activation(y_exp(t), y_t(t), ACT.Copy, scale=col[:, 2:3]).then_inc(y_exp_done, 1)
                if t == 1:
                    act.wait_ge(bias_done, 1)
                    act.activation(bias_parts, bias_sc, ACT.Copy).then_inc(bias_hi_done, 1)
            act.wait_ge(f_amax, 1)
            act.activation(f_keep, bank[0][:], ACT.Copy).then_inc(f_kept, 1)
            act.wait_ge(tail_vec, 9)

            def f_divide(t):
                act.activation(f_div(t), f_keep if t == 0 else bank[t][:], ACT.Copy,
                               scale=col[:, 9:10]).then_inc(f_div_done, 1)

            for t in range(TILES):
                f_divide(t)
                b = {BY_POOL[0] + 2: BY_POOL[0], BY_POOL[1] + 1: BY_POOL[1]}.get(t)
                if b is not None:
                    act.wait_ge(f_clip, b + 1)
                    act.activation(f_div(b), f_div(b), ACT.Copy, scale=col[:, 7:8]).then_inc(f_back, 1)

        @block.tensor
        def _(pe):
            def raise_clock(count):
                for _ in range(count):
                    pe.matmul(bank[7][:], warm[:, 0:P], warm, start=True, stop=True)

            pe.wait_ge(warm_done, 1)
            raise_clock(14)
            for t in range(TILES):
                pe.wait_ge(sel_lhs_pool if t // 2 % 2 else sel_lhs, t // 4 + 1)
                for i in range(3):
                    if t == 0:
                        pe.wait_ge(wc_step, 2 * i + 1)
                    for k in range(4):
                        mm = pe.matmul(sel_ps[t // TPU][:, (t % TPU) * 64:(t % TPU + 1) * 64],
                                       selector[t // 2][:, k, (t % 2) * BPT:(t % 2 + 1) * BPT, :], wc_part[i][:, k, :],
                                       start=(k == 0 and i == 0), stop=(k == 3 and i == 2))
                if t % TPU == TPU - 1:
                    mm.then_inc(sel_mm, 1)
            for t in range(TILES):
                pe.wait_ge(wbd_done, 1 if t < TPU else 3)
                pe.wait_ge(dma_x[t // 2], 16)
                if t >= 3:
                    pe.wait_ge(h_lo_done, t - 2)
                for c in range(KC):
                    mm = pe.matmul(q_ps[t % 3][:, c * P:(c + 1) * P], xacc[:, t, c * P:(c + 1) * P],
                                   wbd1[t // TPU][:, t % TPU, :, :], start=True, stop=True)
                mm.then_inc(h_mm, 1)

            def three_pass(dst, pairs, first_wait=None):
                n = len(pairs)
                for i, ((l_hi, l_lo), (r_hi, r_lo)) in enumerate(pairs):
                    pe.matmul(dst, l_hi, r_hi, start=(i == 0), stop=False)
                    pe.matmul(dst, l_hi, r_lo, start=False, stop=False)
                    mm = pe.matmul(dst, l_lo, r_hi, start=False, stop=(i == n - 1))
                return mm

            def values(i):
                n, t = divmod(i, TILES)
                hi, lo = (wo_hi, wo_lo) if n == 0 else (o_hi, o_lo)
                if t == 0:
                    pe.wait_ge(wv_lo_done, KC * (n + 1))
                pe.wait_ge(h_lo_done, t + 1)
                if i >= 2:
                    pe.wait_ge(v_copied, i - 1)
                rows = slice(t * P, (t + 1) * P)
                three_pass(w_ps[i % 2][:], [((hT_hi[:, c, rows], hT_lo[:, c, rows]), (hi[:, c, :], lo[:, c, :]))
                                            for c in range(KC)]).then_inc(v_mm, 1)

            for i in range(2 * TILES - V_LATE):
                values(i)

            def project(g, r, items):
                u = 2 * g + r
                zero = isinstance(g, int) and u == 0
                rows = slice(r * HALF, (r + 1) * HALF)
                for k in items:
                    n = 2 * ITEMS * g + ITEMS * r + k
                    if r == 0:
                        pe.wait_ge(qk_lo_done, g * ITEMS + k + 1)
                    if not zero:
                        pe.wait_ge(rope_mul, n - 2 if k in (0, 1) else (n - 4 if k == 2 else n - 2))
                    elif k >= 3:
                        pe.wait_ge(rope_mul, n - 2)
                    w = (wk_hi, wk_lo) if k == 0 else (wq_hi, wq_lo)
                    cols = slice(0, HD) if k == 0 else slice((k - 1) * HD, k * HD)
                    three_pass(q_ps[ITEM_BANK[k]][:],
                               [((w[0][:, c, cols], w[1][:, c, cols]), (hT_hi[:, c, rows], hT_lo[:, c, rows]))
                                for c in range(KC)]).then_inc(proj_mm, 1)

            def scores(g, r):
                u = 2 * g + r
                if not (isinstance(g, int) and u == 0):
                    pe.wait_ge(soft_step, SOFT_STEPS * (u - 1) + 1)
                pe.wait_ge(rope_done, ITEMS * (u + 1))
                for j in range(TPU):
                    for b in range(BPT):
                        cols = slice((j * BPT + b) * T, (j * BPT + b + 1) * T)
                        mm = pe.matmul(s_ps[T * b:T * (b + 1), j * P:(j + 1) * P], k_rot[:, cols], q_rot[:, :, cols],
                                       start=True, stop=True)
                mm.then_inc(scores_mm, 1)

            def attend(g, r, j):
                u = 2 * g + r
                if j == 0:
                    pe.wait_ge(p_lo_done, BPT * (u + 1))
                    pe.wait_ge(v_lo_done, 2 * (u + 1))
                if not (isinstance(g, int) and u == 0 and j < 2):
                    pe.wait_ge(o_lo_done, TPU * u + j - 1)
                heads = slice(j * REP, (j + 1) * REP)
                dst = o_ps[j % 2][:].rearrange("p (h b t) -> p h b t", h=REP, b=BPT)
                for i in range(2):
                    pair = dst[:, :, 2 * i:2 * (i + 1), :]
                    pe.matmul(pair, v_st[i][:, j, :], p_st[i][:, heads, :, :], start=True, stop=False)
                    mm = pe.matmul(pair, v_lo[i][:, j, :], p_st[i][:, heads, :, :], start=False, stop=True)
                mm.then_inc(pv_mm, 1)

            def project_out(g, r, j):
                u = 2 * g + r
                if j == 0:
                    pe.wait_ge(wo_lo_done, REP * (g + 1))
                pe.wait_ge(o_lo_done, TPU * u + j + 1)
                if not (isinstance(g, int) and u == 0 and j < 2):
                    pe.wait_ge(acc_done, TPU * u + j - 1)
                elif j == 0:
                    pe.wait_ge(v_copied, 2 * TILES)
                three_pass(w_ps[j % 2][:],
                           [((o_hi[:, j, h * P:(h + 1) * P], o_lo[:, j, h * P:(h + 1) * P]),
                             (wo_hi[:, h, :], wo_lo[:, h, :])) for h in range(REP)]).then_inc(wo_mm, 1)

            def stage(cur, last, late_values=((), ()), early_scores=False):
                project(*cur, range(ITEMS - 1 if last else ITEMS))
                for i in late_values[0]:
                    values(i)
                if last is not None:
                    attend(*last, 0)
                    attend(*last, 1)
                    project(*cur, range(ITEMS - 1, ITEMS))
                    for j in range(2):
                        project_out(*last, j)
                        attend(*last, j + 2)
                        if early_scores and j == 0:
                            scores(*cur)
                if not early_scores:
                    scores(*cur)
                if last is not None:
                    project_out(*last, 2)
                    project_out(*last, 3)
                for i in late_values[1]:
                    values(i)

            late = range(2 * TILES - V_LATE, 2 * TILES)
            stage((0, 0), None, (late[:V_LATE // 2], late[V_LATE // 2:]))
            stage((0, 1), (0, 0))
            with pe.Fori(1, KV - 1) as g:
                stage((g, 0), (g - 1, 1))
                stage((g, 1), (g, 0))
            stage((KV - 1, 0), (KV - 2, 1))
            stage((KV - 1, 1), (KV - 1, 0), early_scores=True)

            def mix2(t):
                pe.wait_ge(acc_done, TPU * 2 * (KV - 1) + t + 1)
                if t == 0:
                    pe.wait_ge(rope_mul, 2 * ITEMS * KV)
                if t >= 3:
                    pe.wait_ge(y_copied, t - 2)
                for c in range(KC):
                    mm = pe.matmul(q_ps[t % 3][:, c * P:(c + 1) * P], xacc[:, t, c * P:(c + 1) * P],
                                   wbd2[:, t, :, :], start=True, stop=True)
                mm.then_inc(y_mm, 1)

            last = (KV - 1, 1)
            for t in range(TPU - 1):
                mix2(t)
            attend(*last, 0)
            attend(*last, 1)
            mix2(TPU - 1)
            project_out(*last, 0)
            attend(*last, 2)
            project_out(*last, 1)
            mix2(TPU)
            attend(*last, 3)
            project_out(*last, 2)
            mix2(TPU + 1)
            project_out(*last, 3)
            mix2(TPU + 2)
            mix2(TPU + 3)
            pe.wait_ge(w8_step, 3 * KC)
            pe.wait_ge(o_lo_done, 2 * TPU * KV)
            for c in range(KC):
                dst = o_ps[c // 2][:].bitcast(BF16)
                for d in range(KC):
                    mm = pe.transpose(dst[:, (c % 2) * 512 + d * P:(c % 2) * 512 + (d + 1) * P],
                                      w8[:, c, d * P:(d + 1) * P], ident_bf[:])
                if c % 2:
                    mm.then_inc(wT_mm, 1)

            def spread_max(n):
                ps = s_ps if n == 0 else q_ps[0]
                pe.wait_ge(tail_vec, 5 * n + 1)
                if n == 1:
                    pe.wait_ge(f_kept, 1)
                pe.transpose(ps[0:1, 0:P], col[:, 4 * n:4 * n + 1], ident).then_inc(tail_mm, 1)
                pe.wait_ge(tail_vec, 5 * n + 2)
                pe.matmul(ps[:, P:P + 1], cst[0:1, C_ONE:C_ONE + P], row[0:1, n:n + 1],
                          start=True, stop=True).then_inc(tail_mm, 1)

            spread_max(0)
            for t in range(TILES):
                if t == 0:
                    pe.wait_ge(wT_done, KC)
                    pe.wait_ge(y8_done, 1)
                    for c in range(KC):
                        pe.matmul(bank[t][:], y8[:, t, c * P:(c + 1) * P], wT[c // 2][:, c % 2, :], start=(c == 0), stop=False)
                    pe.wait_ge(bias_done, 2)
                    pe.matmul(bank[t][:], ones_r[:], bias_parts, start=False, stop=True).then_inc(f_mm, 1)
                else:
                    pe.matmul(bank[t][:], ones_r[:], bias_parts, start=True, stop=False)
                    pe.wait_ge(y8_done, t + 1)
                    for c in range(KC):
                        mm = pe.matmul(bank[t][:], y8[:, t, c * P:(c + 1) * P], wT[c // 2][:, c % 2, :], start=False,
                                       stop=(c == KC - 1))
                    mm.then_inc(f_mm, 1)
            spread_max(1)

        @block.vector
        def _(dve):
            dve.memset(warm, 1.0).then_inc(warm_done, 1)
            dve.memset(ones_r[:].bitcast(F32), 0.0).then_inc(ones_zeroed, 1)
            dve.wait_ge(ones_zeroed, 1)
            dve.memset(ones_r[0:1, :].bitcast(F32), 1.0)
            dve.memset(ones_r[BIAS_ROWS - 1:BIAS_ROWS, :].bitcast(F32), 1.0)
            dve.wait_ge(dma_cond, 64)
            dve.wait_ge(dma_const, 16)
            dve.tensor_copy(tok_f[:], tok_i[:]).then_inc(tok_step, 1)
            dve.wait_ge(tok_step, 1)
            dve.tensor_tensor(tok_eq[:], tok_f[:].unsqueeze(1).broadcast_to([P, 4, BATCH]),
                              cst[:, C_SVAL:C_SVAL + 4].unsqueeze(2).broadcast_to([P, 4, BATCH]),
                              ALU.is_equal).then_inc(tok_step, 1)
            dve.wait_ge(wc_step, 1)
            dve.tensor_tensor(wc_rest, wcond, wc_part[0], ALU.subtract).then_inc(wc_step, 1)
            dve.wait_ge(tok_step, 2)
            select_pair(dve, 0).then_inc(sel_lhs, 1)
            dve.wait_ge(wc_step, 3)
            dve.tensor_tensor(wc_rest, wc_rest, wc_part[1], ALU.subtract).then_inc(wc_step, 1)
            select_pair(dve, 2).then_inc(sel_lhs, 1)
            for half in range(2):
                dve.wait_ge(sel_mm, half + 1)
                picked = sel_ps[half][:, 0:TPU * 64].rearrange("p (t w d) -> p t w d", w=2, d=T)
                for w, dst in enumerate((wbd1[half], wbd2[:, half * TPU:(half + 1) * TPU])):
                    dve.tensor_tensor(dst, picked[:, :, w, :].unsqueeze(2).broadcast_to([P, TPU, BPT, T]), block_b,
                                      ALU.mult).then_inc(wbd_done, 1)

            def h_low(t):
                dve.wait_ge(h_hi_done, t + 1)
                cols = slice(t * P, (t + 1) * P)
                dve.tensor_tensor(hT_lo[:, :, cols], q_ps[t % 3][:].rearrange("p (c r) -> p c r", c=KC),
                                  hT_hi[:, :, cols].bitcast(F32), ALU.subtract).then_inc(h_lo_done, 1)

            for t in range(TILES):
                h_low(t)

            def round_e4m3(dst, scaled, plain, total, done, n):
                dve.tensor_scalar(scaled.bitcast(I32), scaled.bitcast(I32), EXP_BITS, HALF_BIT,
                                  ALU.bitwise_and, ALU.bitwise_or).then_inc(done, 1)
                dve.wait_ge(done, 3 * n + 1)
                dve.scalar_tensor_tensor(out=total, in0=scaled, scalar=LEAST, in1=plain, op0=ALU.max,
                                         op1=ALU.add).then_inc(done, 1)
                dve.wait_ge(done, 3 * n + 2)
                dve.scalar_tensor_tensor(out=dst, in0=scaled, scalar=LEAST, in1=total, op0=ALU.max,
                                         op1=ALU.subtract).then_inc(done, 1)

            def v_copy(i):
                n, t = divmod(i, TILES)
                dve.wait_ge(v_mm, i + 1)
                dve.tensor_copy(v_all[:, t, n * 512:(n + 1) * 512], w_ps[i % 2][:]).then_inc(v_copied, 1)

            for i in range(2 * TILES - V_LATE):
                v_copy(i)
                if TPU <= i < TPU + KC:
                    c = i - TPU
                    dve.wait_ge(w8_scaled, c + 1)
                    round_e4m3(w8[:, c, :], tmp_scaled[c % 2], q_rot[:, c, :], tmp_sum, w8_step, c)

            def rope(g, r, k):
                n = 2 * ITEMS * g + ITEMS * r + k
                b = (ITEMS * r + k) % 2
                dve.wait_ge(swap_done, n + 1)
                if not (isinstance(g, int) and 2 * g + r == 0 and k < 2):
                    dve.wait_ge(rope_done, n - 1)
                dve.tensor_tensor(by_t(q_swap[b][:]), by_t(q_swap[b][:]), sin_b, ALU.mult)
                dve.tensor_tensor(by_t(q_cos[b][:]), by_t(q_ps[ITEM_BANK[k]][:]), cos_b,
                                  ALU.mult).then_inc(rope_mul, 1)

            def soft(g, r, step):
                u = 2 * g + r
                if step == 0:
                    dve.wait_ge(scores_mm, u + 1)
                elif step != 4:
                    dve.wait_ge(soft_step, SOFT_STEPS * u + step)
                if step == 0:
                    op = dve.transpose(s_nat[:].rearrange("p a t -> p (a t)"), s_ps[:])
                elif step == 1:
                    op = dve.tensor_tensor(s_nat[:], s_nat[:], mask_b, ALU.add)
                elif step == 2:
                    op = dve.tensor_reduce(s_max[:], s_nat[:], AX_X, ALU.max)
                elif step == 3:
                    op = dve.tensor_tensor(s_nat[:], s_nat[:], s_max[:].unsqueeze(2).broadcast_to([P, TPU * REP, T]),
                                           ALU.subtract)
                elif step == 4:
                    dve.wait_ge(exp_done, u + 1)
                    op = dve.tensor_reduce(s_sum[:], s_exp[:], AX_X, ALU.add)
                elif step == 5:
                    op = dve.reciprocal(s_rec[:], s_sum[:])
                elif step == 6:
                    op = dve.tensor_tensor(s_nat[:], s_exp[:], s_rec[:].unsqueeze(2).broadcast_to([P, TPU * REP, T]),
                                           ALU.mult)
                elif step == 7:
                    if not (isinstance(g, int) and u == 0):
                        dve.wait_ge(p_hi_done, BPT * u)
                    op = dve.transpose(p_tr[:].rearrange("p a t -> p (a t)"), s_nat[:].rearrange("p a t -> p (a t)"))
                op.then_inc(soft_step, 1)

            def p_low(g, r):
                u = 2 * g + r
                for b in range(BPT):
                    s = slice(T * b, T * b + T)
                    dve.wait_ge(p_hi_done, BPT * u + b + 1)
                    if b == 0 and not (isinstance(g, int) and u == 0):
                        dve.wait_ge(pv_mm, TPU * u)
                    other = (b + 2) % 4
                    dve.tensor_tensor(p_st[b // 2][T * other:T * other + T, :, b % 2, :], p_tr[s, :, :],
                                      p_st[b // 2][s, :, b % 2, :].bitcast(F32), ALU.subtract).then_inc(p_lo_done, 1)

            def o_low(g, r, j):
                u = 2 * g + r
                dve.wait_ge(o_hi_done, TPU * u + j + 1)
                dve.tensor_tensor(o_lo[:, j, :], o_ps[j % 2][:], o_hi[:, j, :].bitcast(F32),
                                  ALU.subtract).then_inc(o_lo_done, 1)

            def accumulate(g, r, j):
                u = 2 * g + r
                tile = r * TPU + j
                dve.wait_ge(wo_mm, TPU * u + j + 1)
                if not (isinstance(g, int) and g == 0):
                    dve.wait_ge(acc_done, TPU * u - TPU)
                dve.tensor_tensor(xacc[:, tile, :], xacc[:, tile, :], w_ps[j % 2][:], ALU.add).then_inc(acc_done, 1)

            def stage(cur, last, late_values=((), ()), early_scores=False):
                for k in range(3):
                    rope(*cur, k)
                if last is not None:
                    o_low(*last, 0)
                rope(*cur, 3)
                if last is not None:
                    o_low(*last, 1)
                rope(*cur, 4)
                for i in late_values[0]:
                    v_copy(i)
                if last is not None:
                    accumulate(*last, 0)
                    o_low(*last, 2)
                    if not early_scores:
                        accumulate(*last, 1)
                        o_low(*last, 3)
                for step in range(4):
                    soft(*cur, step)
                if last is not None:
                    accumulate(*last, 1 if early_scores else 2)
                soft(*cur, 4)
                if early_scores:
                    o_low(*last, 3)
                for step in range(5, SOFT_STEPS):
                    soft(*cur, step)
                if early_scores:
                    accumulate(*last, 2)
                    p_low(*cur)
                    accumulate(*last, 3)
                    return
                if last is not None:
                    accumulate(*last, 3)
                for i in late_values[1]:
                    v_copy(i)
                p_low(*cur)

            late = range(2 * TILES - V_LATE, 2 * TILES)
            stage((0, 0), None, (late[:V_LATE // 2], late[V_LATE // 2:]))
            stage((0, 1), (0, 0))
            with dve.Fori(1, KV - 1) as g:
                stage((g, 0), (g - 1, 1))
                stage((g, 1), (g, 0))
            stage((KV - 1, 0), (KV - 2, 1))
            stage((KV - 1, 1), (KV - 1, 0), early_scores=True)

            def y_largest(t):
                late = t >= TILES - 2
                dve.wait_ge(y_mm if late else y_copied, t + 1)
                dve.tensor_reduce(y_max[:, t:t + 1], q_ps[t % 3][:] if late else y_t(t), AX_X, ALU.max,
                                  apply_absolute_value=True).then_inc(y_amax, 1)

            last = (KV - 1, 1)
            y_largest(0)
            y_largest(1)
            o_low(*last, 0)
            o_low(*last, 1)
            y_largest(2)
            y_largest(3)
            accumulate(*last, 0)
            o_low(*last, 2)
            accumulate(*last, 1)
            o_low(*last, 3)
            y_largest(TPU)
            accumulate(*last, 2)
            y_largest(TPU + 1)
            accumulate(*last, 3)
            y_largest(TPU + 2)
            y_largest(TPU + 3)

            def spread_largest(n, per_tile, ready):
                ps = s_ps if n == 0 else q_ps[0]
                dve.wait_ge(ready, TILES)
                dve.tensor_reduce(col[:, 4 * n:4 * n + 1], per_tile[:], AX_X, ALU.max).then_inc(tail_vec, 1)
                dve.wait_ge(tail_mm, 2 * n + 1)
                dve.tensor_reduce(row[0:1, n:n + 1], ps[0:1, 0:P], AX_X, ALU.max).then_inc(tail_vec, 1)
                dve.wait_ge(tail_mm, 2 * n + 2)
                return ps[:, P:P + 1]

            amax = spread_largest(0, y_max, y_amax)
            dve.tensor_scalar(col[:, 3:4], amax, 1e-12, 1.0 / FP8_MAX, ALU.max, ALU.mult).then_inc(tail_vec, 1)
            dve.wait_ge(tail_vec, 3)
            dve.reciprocal(col[:, 1:2], col[:, 3:4]).then_inc(tail_vec, 1)
            dve.wait_ge(tail_vec, 4)
            dve.tensor_scalar(col[:, 2:3], col[:, 1:2], SHIFT, None, ALU.mult).then_inc(tail_vec, 1)

            def magic(t):
                if t > 0:
                    dve.wait_ge(y_exp_done, t)
                else:
                    dve.wait_ge(bias_step, 1)
                dve.tensor_scalar(y_exp(t).bitcast(I32), y_exp(t).bitcast(I32), EXP_BITS, HALF_BIT,
                                  ALU.bitwise_and, ALU.bitwise_or).then_inc(y8_magic, 1)

            def f_largest(t):
                dve.wait_ge(f_mm, t + 1)
                dve.tensor_reduce(f_max[:, t:t + 1], bank[t][:], AX_X, ALU.max,
                                  apply_absolute_value=True).then_inc(f_amax, 1)

            dve.tensor_scalar(y_exp(0), y_t(0), col[:, 1:2], SHIFT, ALU.mult, ALU.mult).then_inc(bias_step, 1)
            dve.tensor_scalar(col[:, 8:9], col[:, 3:4], wsc[:, 0:1], None, ALU.mult).then_inc(bias_step, 1)
            magic(0)
            dve.wait_ge(bias_step, 2)
            dve.reciprocal(col[0:BIAS_ROWS, 10:11], col[0:BIAS_ROWS, 8:9]).then_inc(bias_step, 1)
            for t in range(TILES):
                dve.wait_ge(y_div_done, t + 1)
                dve.wait_ge(y8_magic, t + 1)
                dve.scalar_tensor_tensor(out=y_sum[t % 2], in0=y_exp(t), scalar=LEAST, in1=y_div(t), op0=ALU.max,
                                         op1=ALU.add).then_inc(y8_sum, 1)
                if t == 0:
                    dve.wait_ge(bias_step, 3)
                    dve.wait_ge(dma_ffn, 32)
                    dve.tensor_scalar(bias_sc, bias_row, col[0:BIAS_ROWS, 10:11], None, ALU.mult).then_inc(bias_done, 1)
                elif t < TILES - 1:
                    magic(t + 1)
                dve.wait_ge(y8_sum, t + 1)
                dve.scalar_tensor_tensor(out=y8[:, t, :], in0=y_exp(t), scalar=LEAST, in1=y_sum[t % 2], op0=ALU.max,
                                         op1=ALU.subtract).then_inc(y8_done, 1)
                if t == 0:
                    dve.tensor_scalar(col[:, 5:6], col[:, 8:9], 1.0 / FP8_MAX, None, ALU.mult).then_inc(bias_step, 1)
                    magic(1)
                    dve.wait_ge(bias_hi_done, 1)
                    low = slice(BIAS_ROWS - 1, BIAS_ROWS)
                    dve.tensor_tensor(bias_parts[low], bias_sc[low], bias_parts[low].bitcast(F32),
                                      ALU.subtract).then_inc(bias_done, 1)
                if t >= 2:
                    f_largest(t - 2)
            f_largest(TILES - 2)
            f_largest(TILES - 1)
            amax = spread_largest(1, f_max, f_amax)
            dve.tensor_scalar(col[:, 7:8], amax, col[:, 5:6], 1e-12 / FP8_MAX, ALU.mult, ALU.max).then_inc(tail_vec, 1)
            dve.wait_ge(tail_vec, 8)
            dve.reciprocal(col[:, 6:7], col[:, 7:8]).then_inc(f_step, 1)
            dve.wait_ge(f_step, 1)
            dve.tensor_scalar(col[:, 9:10], col[:, 6:7], col[:, 8:9], None, ALU.mult).then_inc(tail_vec, 1)

            def clip(t):
                dve.wait_ge(f_div_done, t + 1)
                dve.tensor_scalar(f_div(t), f_div(t), FP8_MAX, -FP8_MAX, ALU.min, ALU.max).then_inc(f_clip, 1)

            def add_back(t):
                dve.wait_ge(f_clip, t + 1)
                dve.scalar_tensor_tensor(out=xacc[:, t, :], in0=f_div(t), scalar=col[:, 7:8], in1=xacc[:, t, :],
                                         op0=ALU.mult, op1=ALU.add).then_inc(result, 1)

            clip(0)
            clip(1)
            add_back(0)
            clip(2)
            clip(3)
            add_back(2)
            clip(4)
            add_back(4)
            clip(5)
            clip(6)
            add_back(5)
            clip(7)
            add_back(6)
            add_back(7)


_INS = ["x", "itok_B_0_15", "L0_cond_weights", "L0_attn_wq", "L0_attn_wk", "L0_attn_wv", "L0_attn_wo",
        "L0_cond2_weights", "L0_ffn_qweight", "L0_ffn_weight_scale", "L0_ffn_bias"]


def kernel(**inputs):
    import concourse.bacc as bacc
    from concourse.bass_utils import run_bass_kernel_spmd

    nc = bacc.Bacc("TRN2", target_bir_lowering=False, num_devices=1)
    arrays, args = {}, []
    for name in _INS:
        a = np.ascontiguousarray(inputs[name])
        if a.ndim == 0:
            a = a.reshape(1)
        arrays[f"in_{name}"] = a
    arrays["in_constants"] = constant_table()
    for name, a in arrays.items():
        args.append(nc.dram_tensor(name, a.shape, mybir.dt.from_np(a.dtype), kind="ExternalInput").ap())
    out = nc.dram_tensor("out_0", (BATCH, T, HID), F32, kind="ExternalOutput").ap()
    build(nc, *args, out)
    r = run_bass_kernel_spmd(nc, [arrays], core_ids=[0])
    return r.results[0]["out_0"]
```
